# Optimizing a Trainium2 kernel written in Bass

```python
import numpy as np
import jax
import jax.numpy as jnp

def _softmax(x, axis=-1):
    return jax.nn.softmax(x, axis=axis)

def _gelu(x):
    return jax.nn.gelu(x, approximate=True)

def _silu(x):
    return jax.nn.silu(x)

def _sigmoid(x):
    return jax.nn.sigmoid(x)

def _layernorm(x, axis=-1, eps=1e-05):
    m = jnp.mean(x, axis=axis, keepdims=True)
    v = jnp.var(x, axis=axis, keepdims=True)
    return (x - m) / jnp.sqrt(v + eps)

def _scatter_add(tgt, idx, src, axis=0):
    return tgt.at[idx].add(src)

def _segment_sum(src, seg, n):
    return jax.ops.segment_sum(src, seg, n)
kernel_name = 'mk_adaln_attn_ffn_d1_seqx_r4_553b1d'

def setup_inputs(seed: int=0):
    np.random.seed(seed)
    _w = jnp.asarray

    def _rec_inputs():
        import jax
        import jax.numpy as jnp
        _rk = jax.random.key(seed)
        x = -0.000125 + 0.9999 * jax.random.normal(jax.random.fold_in(_rk, 1), (8, 512, 256), jnp.float32)
        _lenS = 512 - jax.random.randint(jax.random.fold_in(_rk, 7), (8,), 0, max(1, 512 // 4) + 1, jnp.int32)
        _lenS2 = 512 - jax.random.randint(jax.random.fold_in(_rk, 8), (8,), 0, max(1, 512 // 4) + 1, jnp.int32)
        cond_1024 = -0.00493535 + 1.00056 * jax.random.normal(jax.random.fold_in(_rk, 11), (8, 256), jnp.float32)
        return (x, cond_1024)
    x, cond_1024 = _rec_inputs()

    def _L0_cond_setup():
        import jax, jax.numpy as jnp
        import numpy as np
        N, T, D, H = (64, 128, 256, 256)
        key = jax.random.key(seed)
        k1, k2, k3, k4 = jax.random.split(key, 4)
        x = jax.random.normal(k1, (N, T, D), dtype=jnp.float32)
        h0 = jax.random.normal(k2, (N, H), dtype=jnp.float32)
        Wx = jax.random.normal(k3, (D, H), dtype=jnp.float32) / jnp.sqrt(jnp.float32(D))
        Wh = jax.random.normal(k4, (H, H), dtype=jnp.float32) / jnp.sqrt(jnp.float32(H))
        b = jnp.zeros((H,), dtype=jnp.float32)
        return {'x': x, 'h0': h0, 'Wx': Wx, 'Wh': Wh, 'b': b}
    _L0_cond_all = _L0_cond_setup()
    _L0_cond_in = {k: v for k, v in _L0_cond_all.items() if k in ('Wx', 'Wh', 'b')}
    del _L0_cond_all

    def _L0_attn_setup():
        import jax, jax.numpy as jnp
        import numpy as np
        B, L, D_MODEL, D_STATE = (8, 1024, 256, 64)
        key = jax.random.key(seed)
        k1, k2, k3, k4 = jax.random.split(key, 4)
        u = jax.random.normal(k1, (B, L, D_MODEL), dtype=jnp.float32)
        A_log = jnp.log(jnp.arange(1, D_STATE + 1, dtype=jnp.float32))
        D = jax.random.normal(k2, (D_MODEL,), dtype=jnp.float32)
        C_re = jax.random.normal(k3, (D_MODEL, D_STATE), dtype=jnp.float32)
        C_im = jax.random.normal(k4, (D_MODEL, D_STATE), dtype=jnp.float32)
        log_dt = jnp.log(jnp.full((D_MODEL,), 0.01, dtype=jnp.float32))
        return {'u': u, 'A_log': A_log, 'D': D, 'C_re': C_re, 'C_im': C_im, 'log_dt': log_dt}
    _L0_attn_all = _L0_attn_setup()
    _L0_attn_in = {k: v for k, v in _L0_attn_all.items() if k in ('A_log', 'D', 'C_re', 'C_im', 'log_dt')}
    del _L0_attn_all

    def _L0_cond2_setup():
        import jax, jax.numpy as jnp
        import numpy as np
        EPS = 1e-08
        key = jax.random.key(seed)
        ks = jax.random.split(key, 8)
        B, S, D, H = (8, 512, 256, 256)
        scale = 1.0 / np.sqrt(D)
        return {'input_seq': jax.random.normal(ks[0], (B, S, D), dtype=jnp.float32), 'initial_hidden': jax.random.normal(ks[1], (B, H), dtype=jnp.float32), 'W_f': jax.random.normal(ks[2], (H, D), dtype=jnp.float32) * scale, 'b_f': jnp.zeros((H,), dtype=jnp.float32), 'W_i': jax.random.normal(ks[3], (H, D), dtype=jnp.float32) * scale, 'b_i': jnp.zeros((H,), dtype=jnp.float32), 'W_h': jax.random.normal(ks[4], (H, D), dtype=jnp.float32) * scale, 'b_h': jnp.zeros((H,), dtype=jnp.float32)}
    _L0_cond2_all = _L0_cond2_setup()
    _L0_cond2_in = {k: v for k, v in _L0_cond2_all.items() if k in ('W_f', 'b_f', 'W_i', 'b_i', 'W_h', 'b_h')}
    del _L0_cond2_all

    def _L0_ffn_setup():
        import jax, jax.numpy as jnp
        import numpy as np
        B, S, D = (1, 512, 256)
        F = 352
        E = 16
        K = 2
        CAP_FACTOR = 1.25

        def _mlp(h, wg, wu, wd):
            return jax.nn.silu(h @ wg) * (h @ wu) @ wd
        key = jax.random.key(seed)
        ks = jax.random.split(key, 10)
        sd = 0.02
        return {'x': jax.random.normal(ks[0], (B, S, D), jnp.float32), 'router_w': jax.random.normal(ks[1], (D, E), jnp.float32) * sd, 'router_b': jnp.zeros((E,), jnp.float32), 'w_gate': jax.random.normal(ks[2], (E, D, F), jnp.float32) * sd, 'w_up': jax.random.normal(ks[3], (E, D, F), jnp.float32) * sd, 'w_down': jax.random.normal(ks[4], (E, F, D), jnp.float32) * sd, 'sw_gate': jax.random.normal(ks[5], (D, F), jnp.float32) * sd, 'sw_up': jax.random.normal(ks[6], (D, F), jnp.float32) * sd, 'sw_down': jax.random.normal(ks[7], (F, D), jnp.float32) * sd}
    _L0_ffn_all = _L0_ffn_setup()
    _L0_ffn_in = {k: v for k, v in _L0_ffn_all.items() if k in ('router_w', 'router_b', 'w_gate', 'w_up', 'w_down', 'sw_gate', 'sw_up', 'sw_down')}
    del _L0_ffn_all
    return {'x': x, 'cond_1024': cond_1024, 'L0_cond_Wx': _L0_cond_in['Wx'], 'L0_cond_Wh': _L0_cond_in['Wh'], 'L0_cond_b': _L0_cond_in['b'], 'L0_attn_A_log': _L0_attn_in['A_log'], 'L0_attn_D': _L0_attn_in['D'], 'L0_attn_C_re': _L0_attn_in['C_re'], 'L0_attn_C_im': _L0_attn_in['C_im'], 'L0_attn_log_dt': _L0_attn_in['log_dt'], 'L0_cond2_W_f': _L0_cond2_in['W_f'], 'L0_cond2_b_f': _L0_cond2_in['b_f'], 'L0_cond2_W_i': _L0_cond2_in['W_i'], 'L0_cond2_b_i': _L0_cond2_in['b_i'], 'L0_cond2_W_h': _L0_cond2_in['W_h'], 'L0_cond2_b_h': _L0_cond2_in['b_h'], 'L0_ffn_router_w': _L0_ffn_in['router_w'], 'L0_ffn_router_b': _L0_ffn_in['router_b'], 'L0_ffn_w_gate': _L0_ffn_in['w_gate'], 'L0_ffn_w_up': _L0_ffn_in['w_up'], 'L0_ffn_w_down': _L0_ffn_in['w_down'], 'L0_ffn_sw_gate': _L0_ffn_in['sw_gate'], 'L0_ffn_sw_up': _L0_ffn_in['sw_up'], 'L0_ffn_sw_down': _L0_ffn_in['sw_down']}

def reference(x, cond_1024, L0_cond_Wx, L0_cond_Wh, L0_cond_b, L0_attn_A_log, L0_attn_D, L0_attn_C_re, L0_attn_C_im, L0_attn_log_dt, L0_cond2_W_f, L0_cond2_b_f, L0_cond2_W_i, L0_cond2_b_i, L0_cond2_W_h, L0_cond2_b_h, L0_ffn_router_w, L0_ffn_router_b, L0_ffn_w_gate, L0_ffn_w_up, L0_ffn_w_down, L0_ffn_sw_gate, L0_ffn_sw_up, L0_ffn_sw_down):
    import jax
    import jax.numpy as jnp

    def _L0_cond_ref(x, h0, Wx, Wh, b):
        import jax, jax.numpy as jnp
        import numpy as np
        N, T, D, H = (64, 128, 256, 256)
        xw = jnp.einsum('ntd,dh->nth', x, Wx) + b

        def step(prev_h, xw_t):
            next_h = jnp.tanh(xw_t + prev_h @ Wh)
            return (next_h, next_h)
        _, hs = jax.lax.scan(step, h0, jnp.swapaxes(xw, 0, 1))
        return jnp.swapaxes(hs, 0, 1)

    def _L0_attn_ref(u, A_log, D, C_re, C_im, log_dt):
        import jax, jax.numpy as jnp
        import numpy as np
        B, L, D_MODEL, D_STATE = (8, 1024, 256, 64)
        L_ = u.shape[1]
        dt = jnp.exp(log_dt)
        A = -jnp.exp(A_log)
        t = jnp.arange(L_, dtype=u.dtype)
        at = dt[:, None, None] * A[None, None, :] * t[None, :, None]
        K = jnp.einsum('mn,mln->ml', C_re, jnp.exp(at))
        u_f = jnp.fft.rfft(u.transpose(0, 2, 1), n=2 * L_)
        k_f = jnp.fft.rfft(K, n=2 * L_)
        y = jnp.fft.irfft(u_f * k_f, n=2 * L_)[..., :L_]
        return y.transpose(0, 2, 1) + u * D

    def _L0_cond2_ref(input_seq, initial_hidden, W_f, b_f, W_i, b_i, W_h, b_h):
        import jax, jax.numpy as jnp
        import numpy as np
        EPS = 1e-08
        forget_gate = jax.nn.sigmoid(jnp.einsum('bsd,hd->bsh', input_seq, W_f) + b_f)
        input_gate = jax.nn.sigmoid(jnp.einsum('bsd,hd->bsh', input_seq, W_i) + b_i)
        gate_sum = forget_gate + input_gate + EPS
        forget_norm = forget_gate / gate_sum
        input_norm = input_gate / gate_sum
        candidate = jnp.einsum('bsd,hd->bsh', input_seq, W_h) + b_h
        new_info = input_norm * candidate
        log_ret = jnp.log(forget_norm + EPS)
        log_cumprod = jnp.cumsum(log_ret, axis=1)
        B, _, H = log_cumprod.shape
        padded = jnp.concatenate([jnp.zeros((B, 1, H), dtype=log_cumprod.dtype), log_cumprod], axis=1)
        scaling = jnp.exp(log_cumprod[:, -1:, :] - padded[:, :-1, :])
        hidden = jnp.cumsum(scaling * new_info, axis=1)
        hidden = hidden + jnp.exp(log_cumprod) * initial_hidden[:, None, :]
        return hidden

    def _L0_ffn_ref(x, router_w, router_b, w_gate, w_up, w_down, sw_gate, sw_up, sw_down):
        import jax, jax.numpy as jnp
        import numpy as np
        B, S, D = (1, 512, 256)
        F = 352
        E = 16
        K = 2
        CAP_FACTOR = 1.25

        def _mlp(h, wg, wu, wd):
            return jax.nn.silu(h @ wg) * (h @ wu) @ wd
        b, s, d = x.shape
        N = b * s
        NK = N * K
        C = int(np.ceil(CAP_FACTOR * NK / E))
        x_tokens = x.reshape(N, d)
        logits = x_tokens @ router_w + router_b
        probs = jax.nn.softmax(logits, axis=-1)
        vals, idx = jax.lax.top_k(probs, K)
        vals = vals / (jnp.sum(vals, axis=-1, keepdims=True) + 1e-09)
        idx_flat = idx.reshape(NK)
        vals_flat = vals.reshape(NK)
        oh_e = jax.nn.one_hot(idx_flat, E, dtype=x.dtype)
        pos = (jnp.cumsum(oh_e, axis=0) * oh_e).sum(axis=1) - 1
        within = (pos < C).astype(x.dtype)
        pos_c = jnp.clip(pos, 0, C - 1).astype(jnp.int32)
        token_ids = jnp.arange(NK) // K
        x_pair = x_tokens[token_ids] * within[:, None]
        expert_inputs = jnp.zeros((E, C, d), x.dtype).at[idx_flat, pos_c].add(x_pair)
        expert_outputs = jax.vmap(_mlp)(expert_inputs, w_gate, w_up, w_down)
        gathered = expert_outputs[idx_flat, pos_c] * (vals_flat * within)[:, None]
        output_tokens = gathered.reshape(N, K, d).sum(axis=1)
        return x + _mlp(x, sw_gate, sw_up, sw_down) + output_tokens.reshape(b, s, d)
    x = x + _L0_attn_ref(_L0_cond_ref(x, cond_1024, L0_cond_Wx, L0_cond_Wh, L0_cond_b), L0_attn_A_log, L0_attn_D, L0_attn_C_re, L0_attn_C_im, L0_attn_log_dt)
    x = x + _L0_ffn_ref(_L0_cond2_ref(x, cond_1024, L0_cond2_W_f, L0_cond2_b_f, L0_cond2_W_i, L0_cond2_b_i, L0_cond2_W_h, L0_cond2_b_h), L0_ffn_router_w, L0_ffn_router_b, L0_ffn_w_gate, L0_ffn_w_up, L0_ffn_w_down, L0_ffn_sw_gate, L0_ffn_sw_up, L0_ffn_sw_down)
    return x

_drawn_inputs = setup_inputs


def setup_inputs(seed=0):
    import zlib

    import numpy as np

    out = dict(_drawn_inputs(seed))
    spreads = {'L0_cond_b': (0.0, 0.1),
     'L0_attn_log_dt': (-4.605170249938965, 0.2),
     'L0_cond2_b_f': (0.0, 0.8),
     'L0_cond2_b_i': (0.0, 0.8),
     'L0_cond2_b_h': (0.0, 0.8),
     'L0_ffn_router_b': (0.0, 0.8)}
    factors = {'L0_ffn_router_w': 8.0,
     'L0_ffn_w_gate': 8.0,
     'L0_ffn_w_up': 8.0,
     'L0_ffn_w_down': 8.0,
     'L0_ffn_sw_gate': 8.0,
     'L0_ffn_sw_up': 8.0,
     'L0_ffn_sw_down': 8.0}
    for name, (base, spread) in spreads.items():
        noise = np.random.default_rng([zlib.crc32(name.encode()), seed]).standard_normal(out[name].shape)
        drawn = base * np.exp(spread * noise) if base else spread * noise
        out[name] = jnp.asarray(drawn.astype(out[name].dtype))
    for name, factor in factors.items():
        out[name] = (out[name] * factor).astype(out[name].dtype)
    return out
```

```python
from contextlib import ExitStack

import concourse.bass as bass
from concourse import mybir

F32 = mybir.dt.float32
I32 = mybir.dt.int32
ACT = mybir.ActivationFunctionType
ALU = mybir.AluOpType
AX = mybir.AxisListType

P = 128
B, S, D = 8, 512, 256
C = D // P
TB = S // P
R = B * TB
Q = 32
J = P // Q
W = D // J
G = 8
NST = 64
NH = NST // Q
NG = D // J
CG = 4
NCH = NG // CG
F = 352
FT = [(0, 128), (128, 128), (256, 96)]
NE, K = 16, 2
CAP = int(-(-1.25 * B * S * K // NE))
CT = CAP // P
HALF = CAP // 2
N = B * S
EPS = 1e-8


def build(nc, x_tok, x_steps, h0_rec, h0_gate, wx_d, wh_d, b_rec, a_bc_d, a_q_d, dt_bc_d, dt_q_d, c_q_d, d_k_d,
          gate_w, gate_b, router_w, router_b, sh_gate, sh_up, sh_down, ex_gate, ex_up, ex_down,
          ident_d, consts_d, iota_t_d, tri_d, resets_d, iota_e_d, out):
    k_pad = nc.dram_tensor("k_pad", [D, 2 * P], F32).ap()
    slots_in = nc.dram_tensor("slots_in", [NE * CAP, D], F32).ap()
    slots_out = nc.dram_tensor("slots_out", [NE * CAP, D], F32).ap()

    with ExitStack() as ctx:
        def sb(name, shape, dt=F32):
            return ctx.enter_context(nc.sbuf_tensor(name, shape, dt))

        def sem(name):
            return ctx.enter_context(nc.semaphore(name))

        xtok = sb("xtok", [P, R, D])
        big = sb("big", [P, R * D])
        uT = big[:, :].rearrange("p (k t b) -> p k t b", k=C, b=B)
        hidT = big[:, :].rearrange("p (c r t) -> p c r t", c=C, t=P)
        tok = sb("tok", [P, R * D])
        u_tok = tok[:, :].rearrange("p (g j r) -> p g j r", j=J, r=R)
        hid_tok = tok[:, :].rearrange("p (r d) -> p r d", d=D)
        mid = sb("mid", [P, R * D])
        x1T = mid[:, :].rearrange("p (c r t) -> p c r t", c=C, t=P)
        arena = sb("arena", [P, 11776])

        wx = sb("wx", [P, C, D])
        wh = sb("wh", [P, C, D])
        brec = sb("brec", [P, C])
        h0r = sb("h0r", [P, C, B])
        h0g = sb("h0g", [P, C, B])
        a_bc = sb("a_bc", [P, NST])
        a_q = sb("a_q", [P, NH])
        dt_bc = sb("dt_bc", [P, NG, J])
        dt_q = sb("dt_q", [P, NG])
        c_q = sb("c_q", [P, NG, NH])
        d_k = sb("d_k", [P, NCH])
        dta_q = sb("dta_q", [P, NG, NH])
        lam = sb("lam", [P, NG, NH])
        gw = sb("gw", [P, 3, C, D])
        gb = sb("gb", [P, 3, C])
        rw = sb("rw", [P, C, NE])
        rb = sb("rb", [P, NE])
        ident = sb("ident", [P, P])
        consts = sb("consts", [P, 8])
        iota_t = sb("iota_t", [P, P])
        tri = sb("tri", [P, 2, P])
        resets = sb("resets", [P, NE, R])
        iota_e = sb("iota_e", [P, 2, NE])
        zero = sb("zero", [P, CT * D])

        xst = sb("xst", [P, 2, C, G, B])
        zt = sb("zt", [P, 2, W])
        hring = sb("hring", [P, 2 * G, C, B])

        def part(at, shape):
            n = 1
            for s in shape:
                n *= s
            v = arena[:, at:at + n]
            if len(shape) == 2:
                return v.rearrange("p (a b) -> p a b", a=shape[0])
            if len(shape) == 3:
                return v.rearrange("p (a b c) -> p a b c", a=shape[0], b=shape[1])
            if len(shape) == 4:
                return v.rearrange("p (a b c d) -> p a b c d", a=shape[0], b=shape[1], c=shape[2])
            return v

        tp = part(0, [2, CG, J, P + NST])
        qx = part(6144, [2, CG * NH, P])
        ust = part(8192, [2, CG, J, R])
        stt = part(9216, [2, CG * NH, R])
        xc = part(9728, [2, CG * NH, R])
        ysb = part(10240, [2, CG, P])
        ctmp = part(11264, [CG * NH, B])
        cblk = part(11328, [2, CG, NH, J])
        ksb = part(11392, [2, P])
        gbuf = part(0, [2, 9, 512])
        rt = part(0, [14, R * NE])
        sm = part(7168, [16, R])
        idx = arena[:, 7680:7680 + 4 * R].bitcast(I32).rearrange("p (k r) -> p k r", k=4)
        wt = part(7808, [2, R])
        lgT = part(8000, [2, 512])
        swg = part(9100, [C, F])
        swu = part(9804, [C, F])
        swd = part(10508, [3, D])
        sact3 = mid[:, 0:1536].rearrange("p (f t) -> p f t", f=3)
        ssil = mid[:, 3072:5120].rearrange("p (z t) -> p z t", z=4)
        xg = mid[:, 0:2560].rearrange("p (z t d) -> p z t d", z=2, t=CT)
        xgT = mid[:, 2560:3840].rearrange("p (c t) -> p c t", c=C)
        eact = mid[:, 3840:5760].rearrange("p (f t) -> p f t", f=3)
        esil = mid[:, 5760:6400].rearrange("p (z t) -> p z t", z=2)
        yo = arena[:, 0:2560].rearrange("p (z t d) -> p z t d", z=2, t=CT)
        ewg = arena[:, 2560:3968].rearrange("p (z c f) -> p z c f", z=2, c=C)
        ewu = arena[:, 3968:5376].rearrange("p (z c f) -> p z c f", z=2, c=C)
        ewd = arena[:, 5376:6912].rearrange("p (z f d) -> p z f d", z=2, f=3)
        NGB = 8
        gath = mid[:, 0:NGB * D].rearrange("p (z d) -> p z d", z=NGB)

        ps = ctx.enter_context(nc.psum_tensor("ps", [P, 8, 512], F32))

        names = """s_const s_x s_ps0 s_zero s_dtm s_dta s_lam s_kq s_kqe s_kc s_kmm s_kev s_kz s_sum s_zt s_h s_xdone s_hist
            s_utr s_uev s_ust s_pa s_pe s_qa s_qe s_tmm s_st s_xc s_qmm s_y s_ytr s_x1 s_c s_out
            s_x1tr s_x1ev s_gmm s_fi s_r s_ap s_q s_w s_hid s_htr s_hev s_hadd s_lg s_lge s_ltr s_z s_e s_cnt s_rank s_idx
            s_sw s_smm s_ssil s_sact s_sdn s_sacc s_sc s_zf
            s_xtr s_xev s_emm s_esil s_eact s_edn s_eev s_comb""".split()
        sems = {n: sem(n) for n in names}
        (s_const, s_x, s_ps0, s_zero, s_dtm, s_dta, s_lam, s_kq, s_kqe, s_kc, s_kmm, s_kev, s_kz, s_sum, s_zt, s_h, s_xdone, s_hist,
         s_utr, s_uev, s_ust, s_pa, s_pe, s_qa, s_qe, s_tmm, s_st, s_xc, s_qmm, s_y, s_ytr, s_x1, s_c, s_out,
         s_x1tr, s_x1ev, s_gmm, s_fi, s_r, s_ap, s_q, s_w, s_hid, s_htr, s_hev, s_hadd, s_lg, s_lge, s_ltr, s_z, s_e, s_cnt, s_rank, s_idx,
         s_sw, s_smm, s_ssil, s_sact, s_sdn, s_sacc, s_sc, s_zf,
         s_xtr, s_xev, s_emm, s_esil, s_eact, s_edn, s_eev, s_comb) = [sems[n] for n in names]
        s_xs = [sem("s_xs0"), sem("s_xs1")]
        s_kst = [sem("s_kst0"), sem("s_kst1")]
        s_t0 = [sem("s_t00"), sem("s_t01")]
        s_yst = [sem("s_yst0"), sem("s_yst1")]
        s_ew = [sem("s_ew0"), sem("s_ew1")]
        s_xg = [sem("s_xg0"), sem("s_xg1")]
        s_g = [sem(f"s_g{i}") for i in range(NGB)]
        block = ctx.enter_context(nc.Block())
        loads = ((wh, wh_d), (wx, wx_d), (h0r, h0_rec), (brec, b_rec), (a_bc, a_bc_d), (a_q, a_q_d),
                 (dt_bc, dt_bc_d), (dt_q, dt_q_d), (c_q, c_q_d), (d_k, d_k_d), (consts, consts_d),
                 (iota_t, iota_t_d), (ident, ident_d), (tri, tri_d), (h0g, h0_gate), (gw, gate_w), (gb, gate_b),
                 (rw, router_w), (rb, router_b), (resets, resets_d), (iota_e, iota_e_d))
        LOADED = 16 * len(loads)

        @block.sync
        def _(sp):
            for dst, src in loads:
                sp.dma_start(dst[:], src).then_inc(s_const, 16)
            for z in range(2):
                sp.dma_start(xst[:, z], x_steps[z]).then_inc(s_xs[z], 16)
            sp.dma_start(xtok[:], x_tok).then_inc(s_x, 16)
            sp.wait_ge(s_zero, 1)
            sp.dma_start(k_pad[:, 0:P].rearrange("(c p) t -> p c t", p=P), zero[:, 0:C * P].rearrange("p (c t) -> p c t", c=C)).then_inc(s_kz, 16)
            for e in range(NE):
                sp.dma_start(slots_in[e * CAP:(e + 1) * CAP].rearrange("(p t) d -> p (t d)", p=P), zero[:]).then_inc(s_zf, 16)
            kv = k_pad[:, P:2 * P].rearrange("(c q j) t -> j c q t", c=J, j=CG)
            with sp.Fori(0, NCH // 2) as i:
                for z in range(2):
                    sp.wait_ge(s_kev, 2 * i + z + 1)
                    for j in range(CG):
                        sp.dma_start(kv[j, :, bass.ds(2 * i + z, 1)].rearrange("c q t -> (c q) t"), ksb[Q * j:Q * j + J, z]).then_inc(s_kst[z], 16)
            with sp.Fori(0, S // G // 2 - 1) as i:
                for z in range(2):
                    sp.wait_ge(s_xdone, 2 * i + z + 1)
                    sp.dma_start(xst[:, z], x_steps[bass.ds(2 * i + 2 + z, 1)].rearrange("o p k t b -> (o p) k t b")).then_inc(s_xs[z], 16)
            for z in range(2):
                sp.wait_ge(s_kst[z], 16 * CG * NCH // 2)
            sp.wait_ge(s_kz, 16)
            kt = bass.AP(k_pad.tensor, 1, [[1, P], [2 * P * NG, J], [2 * P, NG], [1, P]])

            def toeplitz(z, chunk):
                for g in range(CG):
                    sp.dma_start(tp[:, z, g, :, 0:P], kt[:, :, bass.ds(chunk * CG + g, 1), :].rearrange("p j o t -> p j (o t)")).then_inc(s_t0[z], 16)
            for z in range(2):
                toeplitz(z, z)
            with sp.Fori(1, NCH // 2) as i:
                for z in range(2):
                    sp.wait_ge(s_tmm, 2 * i + z - 1)
                    toeplitz(z, 2 * i + z)
            sp.wait_ge(s_hid, 2 * B)
            sp.dma_start(swg, sh_gate).then_inc(s_sw, 16)
            sp.dma_start(swu, sh_up).then_inc(s_sw, 16)
            sp.dma_start(swd, sh_down).then_inc(s_sw, 16)

            def weights(z, e):
                sp.dma_start(ewg[:, z], ex_gate[bass.ds(e, 1)].rearrange("o p c f -> (o p) c f")).then_inc(s_ew[z], 16)
                sp.dma_start(ewu[:, z], ex_up[bass.ds(e, 1)].rearrange("o p c f -> (o p) c f")).then_inc(s_ew[z], 16)
                sp.dma_start(ewd[:, z], ex_down[bass.ds(e, 1)].rearrange("o p c f -> (o p) c f")).then_inc(s_ew[z], 16)

            def inputs(z, e):
                sp.dma_start(xg[:, z], slots_in[bass.ds(e * CAP, CAP)].rearrange("(t p) d -> p t d", p=P)).then_inc(s_xg[z], 16)
            sp.wait_ge(s_idx, 1)
            sp.wait_ge(s_sacc, B)
            for z in range(2):
                weights(z, z)
            sp.wait_ge(s_sc, 16 * R * K)
            for z in range(2):
                inputs(z, z)

            def results(z, e):
                sp.dma_start(slots_out[bass.ds(e * CAP, CAP)].rearrange("(t p) d -> p t d", p=P), yo[:, z]).then_inc(s_yst[z], 16)
            with sp.Fori(0, NE // 2 - 1) as i:
                for z in range(2):
                    sp.wait_ge(s_xtr, 6 * i + 3 * z + 3)
                    inputs(z, 2 * i + z + 2)
                    sp.wait_ge(s_edn, 10 * i + 5 * z + 5)
                    weights(z, 2 * i + z + 2)
                    sp.wait_ge(s_eev, 10 * i + 5 * z + 5)
                    results(z, 2 * i + z)
            for z in range(2):
                sp.wait_ge(s_eev, 5 * (NE - 2 + z) + 5)
                results(z, NE - 2 + z)
            for r in range(R):
                sp.wait_ge(s_comb, 2 * r + 2)
                sp.dma_start(out[:, r], xtok[:, r]).then_inc(s_out, 16)
            sp.wait_ge(s_out, 16 * R)

        @block.gpsimd
        def _(pool):
            pool.memset(zero[:], 0.0).then_inc(s_zero, 1)
            with pool.Fori(0, B) as i:
                for z in range(2):
                    pool.wait_ge(s_zero, 1)
                    pool.wait_ge(s_r, 4 * i + 2 * z + 2)
                    pool.tensor_tensor(gbuf[:, z, 4], gbuf[:, z, 0], gbuf[:, z, 2], ALU.mult).then_inc(s_ap, 1)
                    pool.tensor_tensor(gbuf[:, z, 5], gbuf[:, z, 3], gbuf[:, z, 2], ALU.mult).then_inc(s_ap, 1)
                    pool.wait_ge(s_zero, 1)
                    pool.wait_ge(s_q, 2 * i + z + 1)
                    pool.wait_ge(s_ap, 4 * i + 2 * z + 2)
                    pool.tensor_tensor(gbuf[:, z, 8], gbuf[:, z, 7], gbuf[:, z, 5], ALU.mult).then_inc(s_w, 1)
            for n in range(2 * B):
                b, c = n // 2, n % 2
                pool.wait_ge(s_hev, n + 1)
                pool.tensor_tensor(xtok[:, 4 * b:4 * b + 4, c * P:(c + 1) * P], xtok[:, 4 * b:4 * b + 4, c * P:(c + 1) * P],
                                   hid_tok[:, 4 * b:4 * b + 4, c * P:(c + 1) * P], ALU.add).then_inc(s_hadd, 1)
            pool.wait_ge(s_zf, 16 * NE)
            pool.wait_ge(s_idx, 1)
            for r in range(R):
                for k in range(K):
                    pool.indirect_dma_start(out=slots_in[:, :], out_offset=bass.IndirectOffsetOnAxis(ap=idx[:, k, r:r + 1], axis=0),
                                            in_=hid_tok[:, r, :], in_offset=None, bounds_check=NE * CAP - 1, oob_is_err=False).then_inc(s_sc, 16)
            for z in range(2):
                pool.wait_ge(s_yst[z], 8 * NE)
            for n in range(K * R):
                r, k = n // 2, n % 2
                if n >= NGB:
                    pool.wait_ge(s_comb, n - NGB + 1)
                pool.indirect_dma_start(out=gath[:, n % NGB], out_offset=None, in_=slots_out[:, :],
                                        in_offset=bass.IndirectOffsetOnAxis(ap=idx[:, 2 + k, r:r + 1], axis=0)).then_inc(s_g[n % NGB], 16)

        @block.tensor
        def _(pe):
            pe.wait_ge(s_const, LOADED)
            pe.wait_ge(s_ps0, 1)
            with pe.Fori(0, NCH // 2) as i:
                for z in range(2):
                    pe.wait_ge(s_kqe, 2 * i + z + 1)
                    pe.wait_ge(s_kc, 2 * i + z + 1)
                    for j in range(CG):
                        for h in range(NH):
                            last = nc.tensor.matmul(ps[Q * j:Q * j + J, 2 + z, 0:P], cblk[:, z, j, h], qx[:, z, NH * j + h], start=h == 0, stop=h == NH - 1, tile_position=(0, Q * j))
                    last.then_inc(s_kmm, 1)

            def xpart(bank, t):
                for k in range(C):
                    for j in range(J):
                        last = nc.tensor.matmul(ps[Q * j:Q * j + B, bank, t * W:(t + 1) * W], xst[:, bank, k, t], wx[:, k, j * W:(j + 1) * W],
                                                start=t == 0 and k == 0, stop=False, skip_group_check=True, tile_position=(0, Q * j))
                return last
            pe.wait_ge(s_xs[0], 16)
            for t in range(G):
                last = xpart(0, t)
            last.then_inc(s_xdone, 1)

            def steps(i, bank, more):
                for t in range(G):
                    n = bank * G + t
                    for k in range(C):
                        pe.wait_ge(s_h, 4 * G * i + 2 * n + k + 1)
                        for j in range(J):
                            last = nc.tensor.matmul(ps[Q * j:Q * j + B, bank, t * W:(t + 1) * W], hring[:, (n - 1) % (2 * G), k], wh[:, k, j * W:(j + 1) * W],
                                                    start=False, stop=True, skip_group_check=True, tile_position=(0, Q * j))
                    last.then_inc(s_sum, 1)
                    if more:
                        if t == 0:
                            pe.wait_ge(s_xs[1 - bank], 16 * i + 16 + 16 * bank)
                        last = xpart(1 - bank, t)
                if more:
                    last.then_inc(s_xdone, 1)
            IT = S // G // 2
            with pe.Fori(0, IT - 1) as i:
                for bank in range(2):
                    steps(i, bank, True)
            for bank in range(2):
                steps(IT - 1, bank, bank == 0)

            pe.wait_ge(s_hist, 2 * IT)
            n = 0
            for tb in range(TB):
                for k in range(C):
                    for bq in range(2):
                        if n >= 4:
                            pe.wait_ge(s_uev, n - 3)
                        for b in range(4):
                            last = nc.tensor.transpose(ps[:, 2 + n % 4, b * P:(b + 1) * P], uT[:, k, S - (tb + 1) * P:S - tb * P, 4 * bq + b], ident[:])
                        last.then_inc(s_utr, 1)
                        n += 1

            def own_block(z):
                for g in range(CG):
                    o = (g % 2) * (P + NST)
                    for j in range(J):
                        last = nc.tensor.matmul(ps[Q * j:Q * j + Q, 2 * z + g // 2, o:o + P + NST], ust[:, z, g, j], tp[:, z, g, j],
                                                start=g % 2 == 0, stop=False, skip_group_check=True, tile_position=(0, Q * j))
                last.then_inc(s_tmm, 1)

            def carried(z):
                for g in range(CG):
                    o = (g % 2) * (P + NST)
                    for h in range(NH):
                        for j in range(J):
                            last = nc.tensor.matmul(ps[Q * j:Q * j + Q, 2 * z + g // 2, o:o + P], xc[Q * j:Q * j + Q, z, NH * g + h], qx[Q * j:Q * j + Q, z, NH * g + h],
                                                    start=False, stop=True, skip_group_check=True, tile_position=(Q * j, Q * j))
                last.then_inc(s_qmm, 1)

            def by_time(z):
                for g in range(CG):
                    last = nc.tensor.transpose(ps[:, 4 + z, g * P:(g + 1) * P], ysb[:, z, g], ident[:])
                last.then_inc(s_ytr, 1)
            pe.wait_ge(s_uev, 16)
            with pe.Fori(0, NCH // 2) as i:
                for z in range(2):
                    pe.wait_ge(s_ust, 2 * i + z + 1)
                    pe.wait_ge(s_pe, 2 * i + z + 1)
                    pe.wait_ge(s_t0[z], 16 * CG * i + 16 * CG)
                    own_block(z)
                    pe.wait_ge(s_ps0, 1)
                    pe.wait_ge(s_xc, 2 * i + z + 1)
                    pe.wait_ge(s_qe, 2 * i + z + 1)
                    carried(z)
                    pe.wait_ge(s_y, 2 * i + z + 1)
                    by_time(z)
            n = 0
            for b in range(B):
                for c in range(C):
                    if n == 0:
                        pe.wait_ge(s_x1, NCH)
                    if n >= 2:
                        pe.wait_ge(s_x1ev, n - 1)
                    for tb in range(TB):
                        last = nc.tensor.transpose(ps[:, 6 + n % 2, tb * P:(tb + 1) * P], xtok[:, 4 * b + tb, c * P:(c + 1) * P], ident[:])
                    last.then_inc(s_x1tr, 1)
                    n += 1
            pe.wait_ge(s_x1ev, 2 * B)

            def gates(i, z, wait):
                if wait:
                    pe.wait_ge(s_r, 4 * i + 2 * z - 2)
                for q in range(3):
                    for c in range(C):
                        last = nc.tensor.matmul(ps[:, 3 * z + q, :].rearrange("p (r t) -> p r t", r=TB), gw[:, q, c, z * P:(z + 1) * P], x1T[:, c, bass.ds(TB * i, TB), :], start=c == 0, stop=c == C - 1)
                last.then_inc(s_gmm, 1)
            for z in range(2):
                gates(0, z, False)
            with pe.Fori(1, B) as i:
                for z in range(2):
                    gates(i, z, True)
            n = 0
            for b in range(B):
                for c in range(C):
                    if n == 0:
                        pe.wait_ge(s_hid, 2 * B)
                    if n >= 2:
                        pe.wait_ge(s_hev, n - 1)
                    for tb in range(TB):
                        last = nc.tensor.transpose(ps[:, 6 + n % 2, tb * P:(tb + 1) * P], hidT[:, c, 4 * b + tb, :], ident[:])
                    last.then_inc(s_htr, 1)
                    n += 1
            for b in range(B):
                for c in range(C):
                    last = nc.tensor.matmul(ps[Q * (b % J):Q * (b % J) + NE, b // J, :].rearrange("p (r t) -> p r t", r=TB), rw[:, c], hidT[:, c, 4 * b:4 * b + 4, :],
                                            start=c == 0, stop=c == C - 1, tile_position=(0, Q * (b % J)))
            last.then_inc(s_lg, 1)
            pe.wait_ge(s_lge, 1)
            for q in range(2):
                for tb in range(TB):
                    last = nc.tensor.transpose(ps[:, 2 + q, tb * P:(tb + 1) * P], lgT[:, q, tb * P:(tb + 1) * P], ident[:])
            last.then_inc(s_ltr, 1)
            pe.wait_ge(s_cnt, 1)
            for h in range(2):
                last = nc.tensor.matmul(ps[:, 4 + h, :], tri[:, h], rt[:, 9], start=True, stop=True)
            last.then_inc(s_rank, 1)

            pe.wait_ge(s_sw, 48)
            pe.wait_ge(s_idx, 1)
            pe.wait_ge(s_hev, 2 * B)
            nf = 0
            for b in range(B):
                for f, (f0, fw) in enumerate(FT):
                    if nf >= 2:
                        pe.wait_ge(s_sact, nf - 1)
                    for h, w in enumerate((swg, swu)):
                        for c in range(C):
                            last = nc.tensor.matmul(ps[0:fw, 2 * h + nf % 2, :], w[:, c, f0:f0 + fw], hidT[:, c, 4 * b:4 * b + 4, :].rearrange("p r t -> p (r t)"), start=c == 0, stop=c == C - 1)
                    last.then_inc(s_smm, 1)
                    nf += 1
                pe.wait_ge(s_sact, nf)
                if b >= 1:
                    pe.wait_ge(s_sacc, b)
                for tb in range(TB):
                    for f, (f0, fw) in enumerate(FT):
                        last = nc.tensor.matmul(ps[:, 4 + tb // 2, (tb % 2) * D:(tb % 2 + 1) * D], sact3[0:fw, f, tb * P:(tb + 1) * P], swd[0:fw, f], start=f == 0, stop=f == 2)
                last.then_inc(s_sdn, 1)

            def expert(i, z, first):
                pe.wait_ge(s_xg[z], 16 * i + 16)
                units = [[(0, t, t) for t in range(4)], [(1, t, t) for t in range(4)], [(0, 4, 0), (1, 4, 1)]]
                for u, tiles in enumerate(units):
                    if not (first and u < 2):
                        pe.wait_ge(s_xev, 6 * i + 3 * z + u - 1)
                    for c, t, at in tiles:
                        last = nc.tensor.transpose(ps[:, 6 + (z + u) % 2, at * P:(at + 1) * P], xg[:, z, t, c * P:(c + 1) * P], ident[:])
                    last.then_inc(s_xtr, 1)
                pe.wait_ge(s_xev, 6 * i + 3 * z + 3)
                pe.wait_ge(s_ew[z], 48 * i + 48)
                for m in range(6):
                    hf, f = m // 3, m % 3
                    f0, fw = FT[f]
                    if not (first and m < 2):
                        pe.wait_ge(s_eact, 12 * i + 6 * z + m - 1)
                    for h, w in enumerate((ewg, ewu)):
                        for c in range(C):
                            last = nc.tensor.matmul(ps[0:fw, 2 * h + m % 2, 0:HALF], w[:, z, c, f0:f0 + fw], xgT[:, c, hf * HALF:(hf + 1) * HALF], start=c == 0, stop=c == C - 1)
                    last.then_inc(s_emm, 1)
                pe.wait_ge(s_eact, 12 * i + 6 * z + 6)
                for t in range(CT):
                    if not (first and t < 2):
                        pe.wait_ge(s_eev, 10 * i + 5 * z + t - 1)
                    for f, (f0, fw) in enumerate(FT):
                        last = nc.tensor.matmul(ps[:, 4 + (z + t) % 2, 0:D], eact[0:fw, f, t * P:(t + 1) * P], ewd[0:fw, z, f], start=f == 0, stop=f == 2)
                    last.then_inc(s_edn, 1)
            expert(0, 0, True)
            expert(0, 1, False)
            with pe.Fori(1, NE // 2) as i:
                for z in range(2):
                    expert(i, z, False)

        @block.scalar
        def _(act):
            act.preload_act_table(ACT.Tanh)
            act.wait_ge(s_const, LOADED)
            nc.scalar.activation(a_bc[:], a_bc[:], ACT.Exp).then_inc(s_dtm, 1)
            nc.scalar.activation(a_q[:], a_q[:], ACT.Exp).then_inc(s_dtm, 1)
            nc.scalar.activation(dt_bc[:], dt_bc[:], ACT.Exp).then_inc(s_dtm, 1)
            nc.scalar.activation(dt_q[:], dt_q[:], ACT.Exp).then_inc(s_dtm, 1)
            act.wait_ge(s_dta, 1)
            nc.scalar.activation(lam[:], dta_q[:], ACT.Exp, scale=-float(P)).then_inc(s_lam, 1)
            with act.Fori(0, NCH // 2) as i:
                for z in range(2):
                    act.wait_ge(s_kq, 2 * i + z + 1)
                    nc.scalar.activation(qx[:, z], qx[:, z], ACT.Exp, scale=-1.0).then_inc(s_kqe, 1)
            with act.Fori(0, S // G // 2) as i:
                for n in range(2 * G):
                    act.wait_ge(s_zt, 2 * G * i + n + 1)
                    for k in range(C):
                        nc.scalar.activation(hring[:, n, k], zt[:, n % 2, k * Q:k * Q + B], ACT.Tanh, bias=brec[:, k:k + 1]).then_inc(s_h, 1)
            with act.Fori(0, NCH // 2) as i:
                for z in range(2):
                    act.wait_ge(s_pa, 2 * i + z + 1)
                    nc.scalar.activation(tp[:, z, :, :, P:P + NST], tp[:, z, :, :, P:P + NST], ACT.Exp, scale=consts[:, 4:5]).then_inc(s_pe, 1)
                    act.wait_ge(s_qa, 2 * i + z + 1)
                    nc.scalar.activation(qx[:, z], qx[:, z], ACT.Exp, scale=-1.0).then_inc(s_qe, 1)
                    act.wait_ge(s_qmm, 2 * i + z + 1)
                    for hb in range(2):
                        last = nc.scalar.activation(ysb[:, z, 2 * hb:2 * hb + 2], ps[:, 2 * z + hb, 0:2 * (P + NST)].rearrange("p (g t) -> p g t", g=2)[:, :, 0:P], ACT.Copy)
                    last.then_inc(s_y, 1)
            act.preload_act_table(ACT.Sigmoid)

            def gates(i, z, wait):
                act.wait_ge(s_gmm, 2 * i + z + 1)
                if wait:
                    act.wait_ge(s_hid, 2 * i + z - 1)
                for q in range(2):
                    nc.scalar.activation(gbuf[:, z, q], ps[:, 3 * z + q, :], ACT.Sigmoid, bias=gb[:, q, z:z + 1]).then_inc(s_fi, 1)
            for z in range(2):
                gates(0, z, False)
            with act.Fori(1, B) as i:
                for z in range(2):
                    gates(i, z, True)
            act.wait_ge(s_lg, 1)
            act.wait_ge(s_hid, 2 * B)
            nc.scalar.activation(lgT, ps[:, 0:2, :], ACT.Copy).then_inc(s_lge, 1)
            act.wait_ge(s_z, 1)
            nc.scalar.activation(rt[:, 1], rt[:, 1], ACT.Exp).then_inc(s_e, 1)
            act.preload_act_table(ACT.Silu)
            for nf in range(3 * B):
                fw = FT[nf % 3][1]
                act.wait_ge(s_smm, nf + 1)
                if nf >= 2:
                    act.wait_ge(s_sact, nf - 1)
                nc.scalar.activation(ssil[0:fw, nf % 2], ps[0:fw, nf % 2, :], ACT.Silu).then_inc(s_ssil, 1)

            def expert(i, z, first):
                for m in range(6):
                    fw = FT[m % 3][1]
                    act.wait_ge(s_emm, 12 * i + 6 * z + m + 1)
                    if not (first and m < 2):
                        act.wait_ge(s_eact, 12 * i + 6 * z + m - 1)
                    nc.scalar.activation(esil[0:fw, m % 2], ps[0:fw, m % 2, 0:HALF], ACT.Silu).then_inc(s_esil, 1)
                for t in range(CT):
                    act.wait_ge(s_edn, 10 * i + 5 * z + t + 1)
                    if t == 0 and not first_two(i, z, first):
                        act.wait_ge(s_yst[z], 16 * i)
                    nc.scalar.activation(yo[:, z, t], ps[:, 4 + (z + t) % 2, 0:D], ACT.Copy).then_inc(s_eev, 1)

            def first_two(i, z, first):
                return isinstance(i, int) and i == 0
            expert(0, 0, True)
            expert(0, 1, False)
            with act.Fori(1, NE // 2) as i:
                for z in range(2):
                    expert(i, z, False)

        @block.vector
        def _(dve):
            chain = [0]

            def link(ins):
                ins.then_inc(s_c, 1)
                chain[0] = chain[0] + 1
                dve.wait_ge(s_c, chain[0])

            nc.vector.memset(ps[:, 0:4], 0.0).then_inc(s_ps0, 1)
            dve.wait_ge(s_const, LOADED)
            nc.vector.memset(xc[:], 0.0)
            nc.vector.tensor_copy(hring[:, 2 * G - 1], h0r[:]).then_inc(s_h, 2)
            dve.wait_ge(s_dtm, 4)
            nc.vector.tensor_tensor(dta_q[:], dt_q[:].unsqueeze(2).to_broadcast([P, NG, NH]), a_q[:].unsqueeze(1).to_broadcast([P, NG, NH]), ALU.mult).then_inc(s_dta, 1)
            dve.wait_ge(s_dta, 1)

            def decays(z, chunk, done):
                d = dta_q[:, bass.ds(CG * chunk, CG), :].rearrange("p g h -> p (g h)")
                nc.vector.tensor_tensor(qx[:, z], d.unsqueeze(2).to_broadcast([P, CG * NH, P]), iota_t[:].unsqueeze(1).to_broadcast([P, CG * NH, P]), ALU.mult).then_inc(done, 1)

            def kernel_rows(i, z, wait):
                if wait:
                    dve.wait_ge(s_kmm, 2 * i + z - 1)
                decays(z, 2 * i + z, s_kq)
                c = c_q[:, bass.ds(CG * (2 * i + z), CG), :].rearrange("p g h -> p (g h)")
                nc.vector.tensor_tensor(cblk[:, z].rearrange("p g h j -> p (g h) j"), c.unsqueeze(2).to_broadcast([P, CG * NH, J]), consts[:, 0:J].unsqueeze(1).to_broadcast([P, CG * NH, J]), ALU.mult).then_inc(s_kc, 1)

            def kernel_out(i, z, wait):
                dve.wait_ge(s_kmm, 2 * i + z + 1)
                if wait:
                    dve.wait_ge(s_kst[z], 16 * CG * i)
                nc.vector.tensor_scalar(ksb[:, z, 1:P], ps[:, 2 + z, 1:P], 1.0, None, ALU.mult)
                nc.vector.tensor_tensor(ksb[:, z, 0:1], ps[:, 2 + z, 0:1], d_k[:, bass.ds(2 * i + z, 1)], ALU.add).then_inc(s_kev, 1)
            for z in range(2):
                kernel_rows(0, z, False)
            for z in range(2):
                kernel_out(0, z, False)
            with dve.Fori(1, NCH // 2) as i:
                for z in range(2):
                    kernel_rows(i, z, True)
                for z in range(2):
                    kernel_out(i, z, True)

            IT = S // G // 2

            def keep(i, half):
                dve.wait_ge(s_h, 4 * G * i + 2 * G * half + 2 * G + 2)
                nc.vector.tensor_scalar(uT[:, :, bass.ds(i * (-2 * G) + (S - G - G * half), G), :], hring[:, G * half:G * half + G][:, ::-1].rearrange("p t k b -> p k t b"), 1.0, None, ALU.mult).then_inc(s_hist, 1)

            def turn(i, n):
                dve.wait_ge(s_sum, 2 * G * i + n + 1)
                bank, t = n // G, n % G
                nc.vector.transpose(zt[:, n % 2], ps[:, bank, t * W:(t + 1) * W]).then_inc(s_zt, 1)
            with dve.Fori(0, IT) as i:
                for n in range(2 * G):
                    turn(i, n)
                    if n == G:
                        keep(i, 0)
                keep(i, 1)
            n = 0
            for tb in range(TB):
                for k in range(C):
                    for bq in range(2):
                        dve.wait_ge(s_utr, n + 1)
                        for j in range(J):
                            last = nc.vector.tensor_copy(u_tok[:, Q * k:Q * k + Q, j, :].rearrange("p g (b t) -> p g b t", t=TB)[:, :, 4 * bq:4 * bq + 4, tb],
                                                         ps[:, 2 + n % 4, :].rearrange("p (b j g) -> p j g b", b=4, j=J)[:, j])
                        last.then_inc(s_uev, 1)
                        n += 1

            def prepare(i, z, wait):
                chunk = 2 * i + z
                if wait:
                    dve.wait_ge(s_tmm, 2 * i + z - 1)
                nc.vector.tensor_scalar(ust[:, z].rearrange("p g j r -> p (g j r)"), u_tok[:, bass.ds(CG * chunk, CG)].rearrange("p g j r -> p (g j r)"), 1.0, None, ALU.mult).then_inc(s_ust, 1)
                nc.vector.tensor_tensor(tp[:, z, :, :, P:P + NST].rearrange("p g j n -> p (g j) n"), dt_bc[:, bass.ds(CG * chunk, CG), :].rearrange("p g j -> p (g j)").unsqueeze(2).to_broadcast([P, CG * J, NST]),
                                        a_bc[:].unsqueeze(1).to_broadcast([P, CG * J, NST]), ALU.mult).then_inc(s_pa, 1)
                if wait:
                    dve.wait_ge(s_qmm, 2 * i + z - 1)
                decays(z, chunk, s_qa)

            def carry(i, z):
                chunk = 2 * i + z
                dve.wait_ge(s_tmm, 2 * i + z + 1)
                for hb in range(2):
                    last = nc.vector.transpose(stt[:, z].rearrange("p (hb gn) r -> p hb (gn r)", hb=2)[:, hb].rearrange("p (g n) -> p g n", g=2),
                                               ps[:, 2 * z + hb, 0:2 * (P + NST)].rearrange("p (g t) -> p g t", g=2)[:, :, P:P + NST])
                link(last)
                sv = stt[:, z].rearrange("p n (b t) -> p n b t", t=TB)
                lv = lam[:, bass.ds(CG * chunk, CG), :].rearrange("p g h -> p (g h)").unsqueeze(2).to_broadcast([P, CG * NH, B])
                for tb in range(1, TB - 1):
                    link(nc.vector.tensor_tensor(ctmp, sv[:, :, :, tb - 1], lv, ALU.mult))
                    link(nc.vector.tensor_tensor(sv[:, :, :, tb], sv[:, :, :, tb], ctmp, ALU.add))
                cv = c_q[:, bass.ds(CG * chunk, CG), :].rearrange("p g h -> p (g h)").unsqueeze(2).unsqueeze(3).to_broadcast([P, CG * NH, B, TB - 1])
                nc.vector.tensor_tensor(xc[:, z].rearrange("p n (b t) -> p n b t", t=TB)[:, :, :, 1:TB], sv[:, :, :, 0:TB - 1], cv, ALU.mult).then_inc(s_xc, 1)

            def add_x(i, z):
                chunk = 2 * i + z
                dve.wait_ge(s_ytr, 2 * i + z + 1)
                for j in range(J):
                    xv = xtok[:, :, bass.ds(NG * j + CG * chunk, CG)].rearrange("p r g -> p g r")
                    last = nc.vector.tensor_tensor(xv, ps[:, 4 + z, :].rearrange("p (g j r) -> p j g r", g=CG, j=J)[:, j], xv, ALU.add)
                last.then_inc(s_x1, 1)
            dve.wait_ge(s_uev, 16)
            dve.wait_ge(s_x, 16)
            PER = 5
            base = chain[0]
            for z in range(2):
                prepare(0, z, False)
            for z in range(2):
                carry(0, z)
            for z in range(2):
                add_x(0, z)
            assert chain[0] == base + 2 * PER
            with dve.Fori(1, NCH // 2) as i:
                chain[0] = i * (2 * PER) + base
                for z in range(2):
                    prepare(i, z, True)
                for z in range(2):
                    carry(i, z)
                for z in range(2):
                    add_x(i, z)
            chain[0] = base + PER * NCH
            for n in range(2 * B):
                b, c = n // 2, n % 2
                dve.wait_ge(s_x1tr, n + 1)
                nc.vector.tensor_copy(x1T[:, c, 4 * b:4 * b + 4, :], ps[:, 6 + n % 2, :].rearrange("p (r t) -> p r t", r=TB)).then_inc(s_x1ev, 1)
            zeros = zero[:, 0:512]

            def gate(i, z):
                v = lambda m: gbuf[:, z, m]
                dve.wait_ge(s_fi, 4 * i + 2 * z + 2)
                link(nc.vector.scalar_tensor_tensor(v(2), v(0), EPS, v(1), ALU.add, ALU.add))
                nc.vector.reciprocal(v(2), v(2)).then_inc(s_r, 1)
                nc.vector.scalar_tensor_tensor(v(3), ps[:, 3 * z + 2, :], gb[:, 2, z:z + 1], v(1), ALU.add, ALU.mult).then_inc(s_r, 1)
                dve.wait_ge(s_ap, 4 * i + 2 * z + 2)
                link(nc.vector.tensor_scalar(v(4), v(4), EPS, None, ALU.add))
                nc.vector.tensor_tensor_scan(v(7)[:, ::-1], v(4)[:, ::-1], zeros, 1.0, ALU.mult, ALU.add).then_inc(s_q, 1)
                nc.vector.tensor_tensor_scan(v(6), v(4), zeros, h0g[:, z, bass.ds(i, 1)], ALU.mult, ALU.add)
                dve.wait_ge(s_w, 2 * i + z + 1)
                link(nc.vector.tensor_tensor_scan(v(7), v(8), zeros, 0.0, ALU.add, ALU.add))
                nc.vector.tensor_tensor(hidT[:, z, bass.ds(TB * i, TB), :].rearrange("p r t -> p (r t)"), v(7), v(6), ALU.add).then_inc(s_hid, 1)
            base = chain[0]
            with dve.Fori(0, B) as i:
                chain[0] = i * 6 + base
                for z in range(2):
                    gate(i, z)
            chain[0] = base + 6 * B
            for n in range(2 * B):
                b, c = n // 2, n % 2
                dve.wait_ge(s_htr, n + 1)
                nc.vector.tensor_copy(hid_tok[:, 4 * b:4 * b + 4, c * P:(c + 1) * P], ps[:, 6 + n % 2, :].rearrange("p (r d) -> p r d", r=TB)).then_inc(s_hev, 1)

            v = lambda m: rt[:, m].rearrange("p (r e) -> p r e", e=NE)
            row = lambda m: sm[:, m]
            wide = lambda m: sm[:, m].unsqueeze(2).to_broadcast([P, R, NE])
            each = lambda a: a.unsqueeze(1).to_broadcast([P, R, NE])
            dve.wait_ge(s_ltr, 1)
            for q in range(2):
                for tb in range(TB):
                    last = nc.vector.tensor_tensor(v(0).rearrange("p (b t) e -> p b t e", t=TB)[:, J * q:J * q + J, tb], ps[:, 2 + q, tb * P:(tb + 1) * P].rearrange("p (j e) -> p j e", j=J)[:, :, 0:NE],
                                                   rb[:].unsqueeze(1).to_broadcast([P, J, NE]), ALU.add)
            link(last)
            link(nc.vector.tensor_reduce(row(0), v(0), AX.X, ALU.max))
            nc.vector.tensor_tensor(v(1), v(0), wide(0), ALU.subtract).then_inc(s_z, 1)
            dve.wait_ge(s_e, 1)
            link(nc.vector.tensor_reduce(row(1), v(1), AX.X, ALU.add))
            link(nc.vector.reciprocal(row(2), row(1)))
            link(nc.vector.tensor_tensor(v(2), v(1), wide(2), ALU.mult))
            for k in range(K):
                p, val, at, eq, oh = 2 + 4 * k, 3 + k, 5 + k, 3, 4 + k
                if k == 1:
                    link(nc.vector.scalar_tensor_tensor(v(p), v(4), -4.0, v(2), ALU.mult, ALU.add))
                link(nc.vector.tensor_reduce(row(val), v(p), AX.X, ALU.max))
                link(nc.vector.tensor_tensor(v(eq), v(p), wide(val), ALU.is_equal))
                link(nc.vector.scalar_tensor_tensor(v(eq), v(eq), -float(NE), each(iota_e[:, 0]), ALU.mult, ALU.add))
                link(nc.vector.tensor_reduce(row(at), v(eq), AX.X, ALU.min))
                link(nc.vector.tensor_tensor(v(oh), each(iota_e[:, 1]), wide(at), ALU.is_equal))
            nc.vector.tensor_tensor(v(9), v(4), v(5), ALU.add).then_inc(s_cnt, 1)
            dve.wait_ge(s_rank, 1)
            by_e = lambda m: rt[:, m].rearrange("p (e r) -> p e r", r=R)
            link(nc.vector.tensor_copy(by_e(7), ps[:, 5, :].rearrange("p (r e) -> p e r", e=NE)))
            link(nc.vector.tensor_tensor_scan(rt[:, 8], resets[:].rearrange("p e r -> p (e r)"), rt[:, 7], 0.0, ALU.mult, ALU.add))
            link(nc.vector.tensor_tensor(rt[:, 8], rt[:, 8], rt[:, 7], ALU.subtract))
            link(nc.vector.tensor_tensor(v(3), ps[:, 4, :].rearrange("p (r e) -> p r e", e=NE), by_e(8).rearrange("p e r -> p r e"), ALU.add))
            for k in range(K):
                link(nc.vector.tensor_tensor(v(10 + k), v(4 + k), v(3), ALU.mult))
                link(nc.vector.tensor_reduce(row(7 + k), v(10 + k), AX.X, ALU.add))
                link(nc.vector.tensor_scalar(row(9), row(7 + k), float(CAP), None, ALU.is_lt))
                nc.vector.tensor_scalar(row(10), row(7 + k), float(CAP - 1), float(NE * CAP), ALU.min, ALU.add)
                link(nc.vector.tensor_tensor(row(11 + k), row(3), row(4), ALU.add))
                link(nc.vector.tensor_scalar(row(11 + k), row(11 + k), 1e-9, None, ALU.add))
                link(nc.vector.reciprocal(row(11 + k), row(11 + k)))
                link(nc.vector.tensor_tensor(row(11 + k), row(11 + k), row(3 + k), ALU.mult))
                link(nc.vector.tensor_tensor(wt[:, k], row(11 + k), row(9), ALU.mult))
                link(nc.vector.scalar_tensor_tensor(row(13), row(5 + k), float(CAP), row(10), ALU.mult, ALU.add))
                nc.vector.tensor_copy(idx[:, 2 + k], row(13))
                link(nc.vector.tensor_scalar(row(14), row(9), -float(2 * NE * CAP), float(2 * NE * CAP), ALU.mult, ALU.add))
                link(nc.vector.tensor_tensor(row(15), row(14), row(13), ALU.add))
                last = nc.vector.tensor_copy(idx[:, k], row(15))
            last.then_inc(s_idx, 1)

            for b in range(B):
                for f, (f0, fw) in enumerate(FT):
                    nf = 3 * b + f
                    dve.wait_ge(s_ssil, nf + 1)
                    if b >= 1:
                        dve.wait_ge(s_sdn, b)
                    nc.vector.tensor_tensor(sact3[0:fw, f], ssil[0:fw, nf % 2], ps[0:fw, 2 + nf % 2, :], ALU.mult).then_inc(s_sact, 1)
                dve.wait_ge(s_sdn, b + 1)
                dve.wait_ge(s_hadd, 2 * b + 2)
                for q in range(2):
                    last = nc.vector.tensor_tensor(xtok[:, 4 * b + 2 * q:4 * b + 2 * q + 2, :], ps[:, 4 + q, :].rearrange("p (r d) -> p r d", r=2), xtok[:, 4 * b + 2 * q:4 * b + 2 * q + 2, :], ALU.add)
                last.then_inc(s_sacc, 1)

            def expert(i, z, first):
                for u in range(3):
                    dve.wait_ge(s_xtr, 6 * i + 3 * z + u + 1)
                    if u == 0 and not first:
                        dve.wait_ge(s_emm, 12 * i + 6 * z)
                    pv = ps[:, 6 + (z + u) % 2]
                    if u < 2:
                        ins = nc.vector.tensor_copy(xgT[:, u, 0:4 * P], pv)
                    else:
                        ins = nc.vector.tensor_copy(xgT[:, :, 4 * P:5 * P], pv[:, 0:2 * P].rearrange("p (c t) -> p c t", c=C))
                    ins.then_inc(s_xev, 1)
                for m in range(6):
                    hf, f = m // 3, m % 3
                    fw = FT[f][1]
                    dve.wait_ge(s_esil, 12 * i + 6 * z + m + 1)
                    if m == 0 and not first:
                        dve.wait_ge(s_edn, 10 * i + 5 * z)
                    nc.vector.tensor_tensor(eact[0:fw, f, hf * HALF:(hf + 1) * HALF], esil[0:fw, m % 2], ps[0:fw, 2 + m % 2, 0:HALF], ALU.mult).then_inc(s_eact, 1)
            expert(0, 0, True)
            expert(0, 1, False)
            with dve.Fori(1, NE // 2) as i:
                for z in range(2):
                    expert(i, z, False)
            for n in range(K * R):
                r, k = n // 2, n % 2
                dve.wait_ge(s_g[n % NGB], 16 * (n // NGB) + 16)
                if k == 1:
                    dve.wait_ge(s_comb, n)
                nc.vector.scalar_tensor_tensor(xtok[:, r], gath[:, n % NGB], wt[:, k, r:r + 1], xtok[:, r], ALU.mult, ALU.add).then_inc(s_comb, 1)




def kernel(x, cond_1024, L0_cond_Wx, L0_cond_Wh, L0_cond_b, L0_attn_A_log, L0_attn_D, L0_attn_C_re, L0_attn_C_im,
           L0_attn_log_dt, L0_cond2_W_f, L0_cond2_b_f, L0_cond2_W_i, L0_cond2_b_i, L0_cond2_W_h, L0_cond2_b_h,
           L0_ffn_router_w, L0_ffn_router_b, L0_ffn_w_gate, L0_ffn_w_up, L0_ffn_w_down, L0_ffn_sw_gate,
           L0_ffn_sw_up, L0_ffn_sw_down):
    import numpy as np
    import concourse.bacc as bacc
    from concourse.bass_utils import run_bass_kernel_spmd

    f32 = np.float32

    def rows(w):
        return np.asarray(w).reshape(C, P, -1).transpose(1, 0, 2)

    def rec(w):
        return np.asarray(w).reshape(J, C, Q, -1).transpose(0, 2, 1, 3).reshape(P, C, -1)

    def down(w):
        w = np.asarray(w)
        w = np.concatenate([w, np.zeros((3 * P - F, D), f32)])
        return w.reshape(3, P, D).transpose(1, 0, 2)

    x = np.asarray(x)
    cond = np.asarray(cond_1024)
    a_log, c_re, dt = np.asarray(L0_attn_A_log), np.asarray(L0_attn_C_re), np.asarray(L0_attn_log_dt)
    d_k = np.zeros((J, Q, NCH), f32)
    d_k[:, :J] = np.asarray(L0_attn_D).reshape(J, NCH, CG).transpose(2, 0, 1)
    consts = np.zeros((P, 8), f32)
    consts[np.arange(P), np.arange(P) // Q] = 1
    consts[:, 4] = -(np.arange(P) + 1)
    resets = np.ones((P, NE, R), f32)
    resets[:, :, 0] = 0
    iota_e = np.stack([np.arange(NE), np.arange(NE) - NE]).astype(f32)
    tri = np.stack([np.triu(np.ones((P, P)), 1), np.ones((P, P))], 1).astype(f32)
    arrays = {
        "x_tok": x.reshape(B, TB, P, D).transpose(2, 0, 1, 3).reshape(P, R, D),
        "x_steps": x.reshape(B, S // G, G, C, P).transpose(1, 4, 3, 2, 0),
        "h0_rec": rec(cond.T),
        "h0_gate": rows(cond.T),
        "wx": rows(L0_cond_Wx),
        "wh": rec(L0_cond_Wh),
        "b_rec": rec(np.asarray(L0_cond_b)[:, None])[:, :, 0],
        "a_bc": np.broadcast_to(a_log, (P, NST)),
        "a_q": np.tile(a_log.reshape(NH, Q).T, (J, 1)),
        "dt_bc": np.broadcast_to(dt.reshape(J, NG).T, (P, NG, J)),
        "dt_q": np.repeat(dt.reshape(J, NG), Q, 0),
        "c_q": c_re.reshape(J, NG, NH, Q).transpose(0, 3, 1, 2).reshape(P, NG, NH),
        "d_k": d_k.reshape(P, NCH),
        "gate_w": np.stack([rows(np.asarray(w).T) for w in (L0_cond2_W_f, L0_cond2_W_i, L0_cond2_W_h)], 1),
        "gate_b": np.stack([np.asarray(v).reshape(C, P).T for v in (L0_cond2_b_f, L0_cond2_b_i, L0_cond2_b_h)], 1),
        "router_w": rows(L0_ffn_router_w),
        "router_b": np.broadcast_to(np.asarray(L0_ffn_router_b), (P, NE)),
        "sh_gate": rows(L0_ffn_sw_gate),
        "sh_up": rows(L0_ffn_sw_up),
        "sh_down": down(L0_ffn_sw_down),
        "ex_gate": np.stack([rows(w) for w in np.asarray(L0_ffn_w_gate)]),
        "ex_up": np.stack([rows(w) for w in np.asarray(L0_ffn_w_up)]),
        "ex_down": np.stack([down(w) for w in np.asarray(L0_ffn_w_down)]),
        "ident": np.eye(P, dtype=f32),
        "consts": consts,
        "iota_t": np.broadcast_to(np.arange(P, dtype=f32), (P, P)),
        "tri": tri,
        "resets": resets,
        "iota_e": np.broadcast_to(iota_e, (P, 2, NE)),
    }
    arrays = {"in_" + n: np.ascontiguousarray(a) for n, a in arrays.items()}
    nc = bacc.Bacc("TRN2", target_bir_lowering=False, num_devices=1)
    args = [nc.dram_tensor(n, a.shape, mybir.dt.from_np(a.dtype), kind="ExternalInput").ap() for n, a in arrays.items()]
    out = nc.dram_tensor("out", [P, R, D], F32, kind="ExternalOutput").ap()
    build(nc, *args, out)
    got = run_bass_kernel_spmd(nc, [arrays], core_ids=[0]).results[0]["out"]
    return got.reshape(P, B, TB, D).transpose(1, 2, 0, 3).reshape(B, S, D)
```

```python
from contextlib import ExitStack

import concourse.bass as bass
from concourse import mybir

F32 = mybir.dt.float32
I32 = mybir.dt.int32
BF16 = mybir.dt.bfloat16
ACT = mybir.ActivationFunctionType
ALU = mybir.AluOpType
AX = mybir.AxisListType

P = 128
B, S, D = 8, 512, 256
C = D // P
TB = S // P
R = B * TB
Q = 32
J = P // Q
W = D // J
FILL = 256
G = 8
NST = 64
NH = NST // Q
NG = D // J
CG = 4
NCH = NG // CG
F = 352
FT = [(0, 128), (128, 128), (256, 96)]
NE, K = 16, 2
CAP = int(-(-1.25 * B * S * K // NE))
CT = CAP // P
HALF = CAP // 2
N = B * S
EPS = 1e-8
EARLY = 2


def build(nc, x_tok, x_steps, h0_rec, h0_gate, wx_d, wh_d, b_rec_d, a_bc_d, a_q_d, dt_bc_d, dt_q_d, c_q_d, d_k_d,
          gate_w, gate_b, router_w, router_b, sh_gate, sh_up, sh_down, ex_gate, ex_up, ex_down,
          ident_d, consts_d, iota_t_d, tri_d, resets_d, iota_e_d, out):
    k_pad = nc.dram_tensor("k_pad", [D, 2 * P], F32).ap()
    slots_in = nc.dram_tensor("slots_in", [NE * CAP, D], F32).ap()
    slots_out = nc.dram_tensor("slots_out", [NE * CAP, D], F32).ap()

    with ExitStack() as ctx:
        def sb(name, shape, dt=F32):
            return ctx.enter_context(nc.sbuf_tensor(name, shape, dt))

        def sem(name):
            return ctx.enter_context(nc.semaphore(name))

        xtok = sb("xtok", [P, R, D])
        big = sb("big", [P, R * D])
        uT = big[:, :].rearrange("p (k t b) -> p k t b", k=C, b=B)
        hidT = big[:, :].rearrange("p (c r t) -> p c r t", c=C, t=P)
        tok = sb("tok", [P, R * D])
        u_tok = tok[:, :].rearrange("p (g j r) -> p g j r", j=J, r=R)
        hid_tok = tok[:, :].rearrange("p (r d) -> p r d", d=D)
        mid = sb("mid", [P, R * D])
        x1T = mid[:, :].rearrange("p (c r t) -> p c r t", c=C, t=P)
        arena = sb("arena", [P, 11776])

        wx = sb("wx", [P, C, D])
        wh = sb("wh", [P, C, D])
        brow = sb("brow", [1, D])
        h0r = sb("h0r", [P, C, B])
        h0g = sb("h0g", [P, C, B])
        a_bc = sb("a_bc", [P, NST])
        a_q = sb("a_q", [P, NH])
        dt_bc = sb("dt_bc", [P, NG, J])
        dt_q = sb("dt_q", [P, NG])
        c_q = sb("c_q", [P, NG, NH])
        d_k = sb("d_k", [P, NCH])
        dta_q = sb("dta_q", [P, NG, NH])
        lam = sb("lam", [P, NG, NH])
        gw = sb("gw", [P, 3, C, D])
        gb = sb("gb", [P, 3, C])
        rw = sb("rw", [P, C, NE])
        rb = sb("rb", [P, NE])
        ident = sb("ident", [P, P])
        consts = sb("consts", [P, 8])
        iota_t = sb("iota_t", [P, P])
        tri = sb("tri", [P, 2, P])
        resets = sb("resets", [P, NE, R])
        iota_e = sb("iota_e", [P, 2, NE])
        zero = sb("zero", [P, CT * D])

        xst = sb("xst", [P, 2, C, G, B])
        zt = sb("zt", [P, 2, W])
        hring = sb("hring", [P, 2 * G, C, B])

        def part(at, shape):
            n = 1
            for s in shape:
                n *= s
            v = arena[:, at:at + n]
            if len(shape) == 2:
                return v.rearrange("p (a b) -> p a b", a=shape[0])
            if len(shape) == 3:
                return v.rearrange("p (a b c) -> p a b c", a=shape[0], b=shape[1])
            if len(shape) == 4:
                return v.rearrange("p (a b c d) -> p a b c d", a=shape[0], b=shape[1], c=shape[2])
            return v

        tp = part(0, [2, CG, J, P + NST])
        qx = part(6144, [2, CG * NH, P])
        ust = part(8192, [2, CG, J, R])
        stt = part(9216, [2, CG * NH, R])
        xc = part(9728, [2, CG * NH, R])
        ysb = part(10240, [2, CG, P])
        ctmp = part(11264, [CG * NH, B])
        cblk = part(11328, [CG, NH, J])
        ksb = part(11392, [P])
        gbuf = part(0, [2, 8, 512])
        rt = part(0, [14, R * NE])
        sm = part(7168, [16, R])
        idx = arena[:, 7680:7680 + 4 * R].bitcast(I32).rearrange("p (k r) -> p k r", k=4)
        wt = part(7808, [2, R])
        lgT = part(8000, [2, 512])
        swg = part(9100, [C, F])
        swu = part(9804, [C, F])
        swd = part(10508, [3, D])
        sact3 = mid[:, 6400:7936].rearrange("p (f t) -> p f t", f=3)
        sup = mid[:, 3840:4864].rearrange("p (z t) -> p z t", z=2)
        ssil = part(8000, [2, 512])
        xg = mid[:, 0:2560].rearrange("p (z t d) -> p z t d", z=2, t=CT)
        xgT = mid[:, 2560:3840].rearrange("p (c t) -> p c t", c=C)
        eact = mid[:, 3840:5760].rearrange("p (f t) -> p f t", f=3)
        esil = mid[:, 5760:6400].rearrange("p (z t) -> p z t", z=2)
        yo = arena[:, 0:2560].rearrange("p (z t d) -> p z t d", z=2, t=CT)
        ewg = arena[:, 2560:3968].rearrange("p (z c f) -> p z c f", z=2, c=C)
        ewu = arena[:, 3968:5376].rearrange("p (z c f) -> p z c f", z=2, c=C)
        ewd = arena[:, 5376:6912].rearrange("p (z f d) -> p z f d", z=2, f=3)
        NGB = 8
        gath = mid[:, 0:NGB * D].rearrange("p (z d) -> p z d", z=NGB)

        ps = ctx.enter_context(nc.psum_tensor("ps", [P, 8, 512], F32))

        names = """s_const s_x s_ps0 s_zero s_dtm s_dta s_lam s_kq s_kqe s_kc s_kmm s_kev s_sum s_zt s_h s_xdone s_hist
            s_utr s_uev s_ust s_pa s_pe s_qa s_qe s_tmm s_st s_xc s_qmm s_y s_ytr s_x1 s_c s_out
            s_x1tr s_x1ev s_gmm s_fic s_r s_ap s_ip s_new s_q s_w s_cs s_hid s_htr s_hev s_hadd s_lg s_lge s_ltr s_z s_e s_cnt s_rank s_idx
            s_sw s_smm s_ssil s_sact s_sdn s_sacc s_sc s_zf
            s_xtr s_xev s_emm s_esil s_eact s_edn s_eev s_comb""".split()
        sems = {n: sem(n) for n in names}
        (s_const, s_x, s_ps0, s_zero, s_dtm, s_dta, s_lam, s_kq, s_kqe, s_kc, s_kmm, s_kev, s_sum, s_zt, s_h, s_xdone, s_hist,
         s_utr, s_uev, s_ust, s_pa, s_pe, s_qa, s_qe, s_tmm, s_st, s_xc, s_qmm, s_y, s_ytr, s_x1, s_c, s_out,
         s_x1tr, s_x1ev, s_gmm, s_fic, s_r, s_ap, s_ip, s_new, s_q, s_w, s_cs, s_hid, s_htr, s_hev, s_hadd, s_lg, s_lge, s_ltr, s_z, s_e, s_cnt, s_rank, s_idx,
         s_sw, s_smm, s_ssil, s_sact, s_sdn, s_sacc, s_sc, s_zf,
         s_xtr, s_xev, s_emm, s_esil, s_eact, s_edn, s_eev, s_comb) = [sems[n] for n in names]
        s_xs = [sem("s_xs0"), sem("s_xs1")]
        s_kst = sem("s_kst")
        s_late = sem("s_late")
        s_t0 = [sem("s_t00"), sem("s_t01")]
        s_yst = [sem("s_yst0"), sem("s_yst1")]
        s_ew = [sem("s_ew0"), sem("s_ew1")]
        s_xg = [sem("s_xg0"), sem("s_xg1")]
        s_g = [sem(f"s_g{i}") for i in range(NGB)]
        block = ctx.enter_context(nc.Block())
        loads = ((wx, wx_d), (brow, b_rec_d), (tri, tri_d), (wh, wh_d), (h0r, h0_rec), (a_q, a_q_d), (dt_q, dt_q_d), (a_bc, a_bc_d),
                 (dt_bc, dt_bc_d), (c_q, c_q_d), (d_k, d_k_d), (consts, consts_d), (iota_t, iota_t_d))
        late = ((ident, ident_d), (h0g, h0_gate), (gw, gate_w), (gb, gate_b), (rw, router_w), (rb, router_b),
                (resets, resets_d), (iota_e, iota_e_d))
        LOADED, LATE = 16 * len(loads), 16 * len(late)

        @block.sync
        def _(sp):
            for z in range(2):
                sp.dma_start(xst[:, z], x_steps[z]).then_inc(s_xs[z], 16)
            for dst, src in loads:
                sp.dma_start(dst[:], src).then_inc(s_const, 16)
            sp.wait_ge(s_zero, 1)
            sp.dma_start(k_pad[:, 0:P].rearrange("(c p) t -> p c t", p=P), zero[:, 0:C * P].rearrange("p (c t) -> p c t", c=C)).then_inc(s_kst, 16)
            for dst, src in late:
                sp.dma_start(dst[:], src).then_inc(s_late, 16)
            sp.dma_start(xtok[:], x_tok).then_inc(s_x, 16)
            sp.wait_ge(s_kst, 16)
            kv = k_pad[:, P:2 * P].rearrange("(c q j) t -> j c q t", c=J, j=CG)

            def ahead(i, z):
                sp.wait_ge(s_xdone, 2 * i + z + 1)
                sp.dma_start(xst[:, z], x_steps[bass.ds(2 * i + 2 + z, 1)].rearrange("o p k t b -> (o p) k t b")).then_inc(s_xs[z], 16)
            with sp.Fori(0, NCH) as i:
                for z in range(2):
                    ahead(i, z)
                sp.wait_ge(s_kev, i + 1)
                for j in range(CG):
                    sp.dma_start(kv[j, :, bass.ds(i, 1)].rearrange("c q t -> (c q) t"), ksb[Q * j:Q * j + J]).then_inc(s_kst, 16)
            with sp.Fori(NCH, S // G // 2 - 1) as i:
                for z in range(2):
                    ahead(i, z)
            for e in range(NE):
                sp.dma_start(slots_in[e * CAP:(e + 1) * CAP].rearrange("(p t) d -> p (t d)", p=P), zero[:]).then_inc(s_zf, 16)
            sp.wait_ge(s_kst, 16 + 16 * CG * NCH)
            kt = bass.AP(k_pad.tensor, 1, [[1, P], [2 * P * NG, J], [2 * P, NG], [1, P]])

            def toeplitz(z, chunk):
                for g in range(CG):
                    sp.dma_start(tp[:, z, g, :, 0:P], kt[:, :, bass.ds(chunk * CG + g, 1), :].rearrange("p j o t -> p j (o t)")).then_inc(s_t0[z], 16)
            for z in range(2):
                toeplitz(z, z)
            with sp.Fori(1, NCH // 2) as i:
                for z in range(2):
                    sp.wait_ge(s_tmm, 2 * i + z - 1)
                    toeplitz(z, 2 * i + z)
            sp.wait_ge(s_x1, NCH)
            sp.dma_start(swg, sh_gate).then_inc(s_sw, 16)
            sp.dma_start(swu, sh_up).then_inc(s_sw, 16)
            sp.dma_start(swd, sh_down).then_inc(s_sw, 16)

            def weights(z, e):
                sp.dma_start(ewg[:, z], ex_gate[bass.ds(e, 1)].rearrange("o p c f -> (o p) c f")).then_inc(s_ew[z], 16)
                sp.dma_start(ewu[:, z], ex_up[bass.ds(e, 1)].rearrange("o p c f -> (o p) c f")).then_inc(s_ew[z], 16)
                sp.dma_start(ewd[:, z], ex_down[bass.ds(e, 1)].rearrange("o p c f -> (o p) c f")).then_inc(s_ew[z], 16)

            def inputs(z, e):
                sp.dma_start(xg[:, z], slots_in[bass.ds(e * CAP, CAP)].rearrange("(t p) d -> p t d", p=P)).then_inc(s_xg[z], 16)
            sp.wait_ge(s_idx, 1)
            for z in range(2):
                weights(z, z)
            sp.wait_ge(s_sc, 16 * R * K)
            for z in range(2):
                inputs(z, z)

            def results(z, e):
                sp.dma_start(slots_out[bass.ds(e * CAP, CAP)].rearrange("(t p) d -> p t d", p=P), yo[:, z]).then_inc(s_yst[z], 16)
            with sp.Fori(0, NE // 2 - 1) as i:
                for z in range(2):
                    sp.wait_ge(s_xtr, 6 * i + 3 * z + 3)
                    inputs(z, 2 * i + z + 2)
                    sp.wait_ge(s_edn, 10 * i + 5 * z + 5)
                    weights(z, 2 * i + z + 2)
                    sp.wait_ge(s_eev, 10 * i + 5 * z + 5)
                    results(z, 2 * i + z)
            for z in range(2):
                sp.wait_ge(s_eev, 5 * (NE - 2 + z) + 5)
                results(z, NE - 2 + z)
            for r in range(R):
                sp.wait_ge(s_comb, 2 * r + 2)
                sp.dma_start(out[:, r], xtok[:, r]).then_inc(s_out, 16)
            sp.wait_ge(s_out, 16 * R)

        @block.gpsimd
        def _(pool):
            pool.memset(zero[:], 0.0).then_inc(s_zero, 1)

            def decay_args(z, chunk, done):
                d = dta_q[:, bass.ds(CG * chunk, CG), :].rearrange("p g h -> p (g h)")
                pool.tensor_tensor(qx[:, z], d.unsqueeze(2).to_broadcast([P, CG * NH, P]), iota_t[:].unsqueeze(1).to_broadcast([P, CG * NH, P]), ALU.mult).then_inc(done, 1)

            def power_args(z, chunk):
                pool.tensor_tensor(tp[:, z, :, :, P:P + NST].rearrange("p g j n -> p (g j) n"), dt_bc[:, bass.ds(CG * chunk, CG), :].rearrange("p g j -> p (g j)").unsqueeze(2).to_broadcast([P, CG * J, NST]),
                                   a_bc[:].unsqueeze(1).to_broadcast([P, CG * J, NST]), ALU.mult).then_inc(s_pa, 1)
            pool.wait_ge(s_const, LOADED)
            pool.wait_ge(s_dta, 1)
            decay_args(0, 0, s_kq)
            with pool.Fori(1, NCH) as i:
                pool.wait_ge(s_zero, 1)
                pool.wait_ge(s_kmm, i)
                decay_args(0, i, s_kq)
            pool.wait_ge(s_kmm, NCH)
            pool.wait_ge(s_dtm, 4)
            power_args(0, 0)
            power_args(1, 1)
            decay_args(0, 0, s_qa)
            decay_args(1, 1, s_qa)

            def conv_args(s, z):
                pool.wait_ge(s_zero, 1)
                pool.wait_ge(s_tmm, s + 1)
                power_args(z, s + 2)
                pool.wait_ge(s_zero, 1)
                pool.wait_ge(s_qmm, 2 * s + 2)
                decay_args(z, s + 2, s_qa)
            with pool.Fori(0, NCH // 2 - 1) as i:
                for z in range(2):
                    conv_args(2 * i + z, z)
            def gate_products(n, b, z, first):
                v = lambda m: gbuf[:, z, m]
                pool.wait_ge(s_zero, 1)
                pool.wait_ge(s_r, n + 1)
                pool.tensor_tensor(v(4), v(0), v(2), ALU.mult).then_inc(s_ap, 1)
                pool.tensor_tensor(v(5), v(1), v(2), ALU.mult).then_inc(s_ip, 1)
                if not first:
                    hidden_sum(n - 1, b - (1 - z), 1 - z)
                pool.wait_ge(s_zero, 1)
                pool.wait_ge(s_ip, n + 1)
                pool.wait_ge(s_fic, 3 * n + 3)
                pool.tensor_tensor(v(5), v(5), v(3), ALU.mult).then_inc(s_new, 1)
                pool.wait_ge(s_zero, 1)
                pool.wait_ge(s_q, n + 1)
                pool.wait_ge(s_new, n + 1)
                pool.tensor_tensor(v(5), v(5), v(7), ALU.mult).then_inc(s_w, 1)

            def hidden_sum(n, b, z):
                pool.wait_ge(s_zero, 1)
                pool.wait_ge(s_cs, n + 1)
                pool.tensor_tensor(hidT[:, z, bass.ds(TB * b, TB), :].rearrange("p r t -> p (r t)"), gbuf[:, z, 7], gbuf[:, z, 6], ALU.add).then_inc(s_hid, 1)
            for z in range(2):
                gate_products(z, 0, z, z == 0)
            with pool.Fori(1, B) as b:
                for z in range(2):
                    gate_products(2 * b + z, b, z, False)
            hidden_sum(2 * B - 1, B - 1, 1)
            for n in range(2 * B):
                b, c = n // 2, n % 2
                pool.wait_ge(s_hev, n + 1)
                pool.tensor_tensor(xtok[:, 4 * b:4 * b + 4, c * P:(c + 1) * P], xtok[:, 4 * b:4 * b + 4, c * P:(c + 1) * P],
                                   hid_tok[:, 4 * b:4 * b + 4, c * P:(c + 1) * P], ALU.add).then_inc(s_hadd, 1)
            for b in range(EARLY):
                for f, (f0, fw) in enumerate(FT):
                    nf = 3 * b + f
                    pool.wait_ge(s_ssil, nf + 1)
                    if b >= 1:
                        pool.wait_ge(s_sdn, b)
                    pool.tensor_tensor(sact3[0:fw, f], ssil[0:fw, nf % 2], sup[0:fw, nf % 2], ALU.mult).then_inc(s_sact, 1)
            pool.wait_ge(s_zf, 16 * NE)
            pool.wait_ge(s_idx, 1)
            for r in range(R):
                for k in range(K):
                    pool.indirect_dma_start(out=slots_in[:, :], out_offset=bass.IndirectOffsetOnAxis(ap=idx[:, k, r:r + 1], axis=0),
                                            in_=hid_tok[:, r, :], in_offset=None, bounds_check=NE * CAP - 1, oob_is_err=False).then_inc(s_sc, 16)
            for z in range(2):
                pool.wait_ge(s_yst[z], 8 * NE)
            for n in range(K * R):
                r, k = n // 2, n % 2
                if n >= NGB:
                    pool.wait_ge(s_comb, n - NGB + 1)
                pool.indirect_dma_start(out=gath[:, n % NGB], out_offset=None, in_=slots_out[:, :],
                                        in_offset=bass.IndirectOffsetOnAxis(ap=idx[:, 2 + k, r:r + 1], axis=0)).then_inc(s_g[n % NGB], 16)

        @block.tensor
        def _(pe):
            pe.wait_ge(s_const, LOADED)
            pe.wait_ge(s_ps0, 1)
            pe.wait_ge(s_zero, 1)
            zero16 = zero[:].bitcast(BF16)

            def keep_up(columns):
                nc.tensor.matmul(ps[:, 6, 0:columns], zero16[:, 0:P], zero16[:, 0:columns], start=True, stop=True)

            def kernel_sums():
                for h in range(NH):
                    for j in range(CG):
                        last = nc.tensor.matmul(ps[Q * j:Q * j + J, 2, 0:P], cblk[:, j, h], qx[:, 0, NH * j + h], start=h == 0, stop=h == NH - 1, tile_position=(0, Q * j))
                last.then_inc(s_kmm, 1)

            def xpart(bank, t):
                for k in range(C):
                    for j in range(J):
                        nc.tensor.matmul(ps[Q * j:Q * j + B, bank, t * W:(t + 1) * W], xst[:, bank, k, t], wx[:, k, j * W:(j + 1) * W],
                                         start=t == 0 and k == 0, stop=False, skip_group_check=True, tile_position=(0, Q * j))
                for j in range(J):
                    last = nc.tensor.matmul(ps[Q * j:Q * j + B, bank, t * W:(t + 1) * W], tri[0:1, 1, 0:B], brow[:, j * W:(j + 1) * W],
                                            start=False, stop=False, skip_group_check=True, tile_position=(0, Q * j))
                return last
            pe.wait_ge(s_xs[0], 16)
            for t in range(G):
                last = xpart(0, t)
            last.then_inc(s_xdone, 1)

            def steps(i, bank, more, kernel):
                for t in range(G):
                    n = bank * G + t
                    pe.wait_ge(s_h, 2 * G * i + n + 1)
                    for k in range(C):
                        for j in range(J):
                            last = nc.tensor.matmul(ps[Q * j:Q * j + B, bank, t * W:(t + 1) * W], hring[:, (n - 1) % (2 * G), k], wh[:, k, j * W:(j + 1) * W],
                                                    start=False, stop=True, skip_group_check=True, tile_position=(0, Q * j))
                    last.then_inc(s_sum, 1)
                    if more:
                        if t == 0:
                            pe.wait_ge(s_xs[1 - bank], 16 * i + 16 + 16 * bank)
                        last = xpart(1 - bank, t)
                        if t == G - 1:
                            last.then_inc(s_xdone, 1)
                    if kernel and n == 11:
                        pe.wait_ge(s_ps0, 1)
                        pe.wait_ge(s_kqe, i + 1)
                        pe.wait_ge(s_kc, i + 1)
                        kernel_sums()
                    keep_up(FILL)
            IT = S // G // 2
            with pe.Fori(0, NCH) as i:
                for bank in range(2):
                    steps(i, bank, True, True)
            with pe.Fori(NCH, IT - 1) as i:
                for bank in range(2):
                    steps(i, bank, True, False)
            for bank in range(2):
                steps(IT - 1, bank, bank == 0, False)

            pe.wait_ge(s_hist, 2 * IT)
            pe.wait_ge(s_late, LATE)
            n = 0
            for tb in range(TB):
                for k in range(C):
                    for bq in range(2):
                        if n >= 4:
                            pe.wait_ge(s_uev, n - 3)
                        for b in range(4):
                            last = nc.tensor.transpose(ps[:, 2 + n % 4, b * P:(b + 1) * P], uT[:, k, S - (tb + 1) * P:S - tb * P, 4 * bq + b], ident[:])
                        last.then_inc(s_utr, 1)
                        n += 1

            def own_block(s, z, wait):
                pe.wait_ge(s_ust, s + 1)
                pe.wait_ge(s_pe, s + 1)
                pe.wait_ge(s_t0[z], 8 * CG * (s - z) + 16 * CG)
                for g in range(CG):
                    if wait and g % 2 == 0:
                        pe.wait_ge(s_y, 2 * s - 3 + g // 2)
                    o = (g % 2) * (P + NST)
                    for j in range(J):
                        last = nc.tensor.matmul(ps[Q * j:Q * j + Q, 2 * z + g // 2, o:o + P + NST], ust[:, z, g, j], tp[:, z, g, j],
                                                start=g % 2 == 0, stop=False, skip_group_check=True, tile_position=(0, Q * j))
                    if g < CG - 1:
                        keep_up(128)
                last.then_inc(s_tmm, 1)
                keep_up(128)

            def carried(s, z):
                pe.wait_ge(s_ps0, 1)
                pe.wait_ge(s_xc, s + 1)
                pe.wait_ge(s_qe, s + 1)
                for g in range(CG):
                    o = (g % 2) * (P + NST)
                    for h in range(NH):
                        for j in range(J):
                            last = nc.tensor.matmul(ps[Q * j:Q * j + Q, 2 * z + g // 2, o:o + P], xc[Q * j:Q * j + Q, z, NH * g + h], qx[Q * j:Q * j + Q, z, NH * g + h],
                                                    start=False, stop=True, skip_group_check=True, tile_position=(Q * j, Q * j))
                    if g % 2 == 1:
                        last.then_inc(s_qmm, 1)
                    keep_up(128)

            def by_time(s, z, wait):
                pe.wait_ge(s_y, 2 * s + 2)
                if wait:
                    pe.wait_ge(s_x1, s - 1)
                for g in range(CG):
                    last = nc.tensor.transpose(ps[:, 4 + z, g * P:(g + 1) * P], ysb[:, z, g], ident[:])
                last.then_inc(s_ytr, 1)
                for _ in range(2):
                    keep_up(512)
            pe.wait_ge(s_uev, 16)
            own_block(0, 0, False)
            own_block(1, 1, False)
            carried(0, 0)
            for s in (2, 3):
                own_block(s, s % 2, True)
                carried(s - 1, 1 - s % 2)
                by_time(s - 2, s % 2, False)
            with pe.Fori(2, NCH // 2) as i:
                for z in range(2):
                    own_block(2 * i + z, z, True)
                    carried(2 * i + z - 1, 1 - z)
                    by_time(2 * i + z - 2, z, True)
            carried(NCH - 1, 1)
            by_time(NCH - 2, 0, True)
            by_time(NCH - 1, 1, True)
            def x1_turned(b):
                for c in range(C):
                    if b >= 3:
                        pe.wait_ge(s_hev, 2 * (b - 3) + c + 1)
                    elif b >= 1:
                        pe.wait_ge(s_x1ev, 2 * (b - 1) + c + 1)
                    for tb in range(TB):
                        last = nc.tensor.transpose(ps[:, 6 + c, tb * P:(tb + 1) * P], xtok[:, 4 * b + tb, c * P:(c + 1) * P], ident[:])
                    last.then_inc(s_x1tr, 1)

            def hid_turned(b):
                pe.wait_ge(s_hid, 2 * b + 2)
                for c in range(C):
                    pe.wait_ge(s_x1ev, min(2 * (b + 2) + c + 1, 2 * B))
                    if b >= B - 2:
                        pe.wait_ge(s_hev, 2 * (b - 1) + c + 1)
                    for tb in range(TB):
                        last = nc.tensor.transpose(ps[:, 6 + c, tb * P:(tb + 1) * P], hidT[:, c, 4 * b + tb, :], ident[:])
                    last.then_inc(s_htr, 1)
            pe.wait_ge(s_x1, NCH)
            x1_turned(0)
            for b in range(B):
                if b + 1 < B:
                    x1_turned(b + 1)
                pe.wait_ge(s_x1ev, 2 * b + 2)
                for z in range(2):
                    if b >= 1:
                        pe.wait_ge(s_fic, 3 * (2 * b + z) - 3)
                    for q in range(3):
                        for c in range(C):
                            last = nc.tensor.matmul(ps[:, 3 * z + q, :], gw[:, q, c, z * P:(z + 1) * P], x1T[:, c, 4 * b:4 * b + 4, :].rearrange("p r t -> p (r t)"), start=c == 0, stop=c == C - 1)
                    last.then_inc(s_gmm, 1)
                if b >= 1:
                    hid_turned(b - 1)
            hid_turned(B - 1)
            pe.wait_ge(s_fic, 6 * B)
            for b in range(B):
                for c in range(C):
                    last = nc.tensor.matmul(ps[Q * (b % J):Q * (b % J) + NE, b // J, :].rearrange("p (r t) -> p r t", r=TB), rw[:, c], hidT[:, c, 4 * b:4 * b + 4, :],
                                            start=c == 0, stop=c == C - 1, tile_position=(0, Q * (b % J)))
            last.then_inc(s_lg, 1)
            pe.wait_ge(s_lge, 1)
            pe.wait_ge(s_hev, 2 * B)
            for q in range(2):
                for tb in range(TB):
                    last = nc.tensor.transpose(ps[:, 6 + q, tb * P:(tb + 1) * P], lgT[:, q, tb * P:(tb + 1) * P], ident[:])
            last.then_inc(s_ltr, 1)

            pe.wait_ge(s_sw, 48)
            nf = 0
            for b in range(B):
                for f, (f0, fw) in enumerate(FT):
                    if nf >= 2:
                        pe.wait_ge(s_sact, nf - 1)
                    for h, w in enumerate((swg, swu)):
                        for c in range(C):
                            last = nc.tensor.matmul(ps[0:fw, 2 * h + nf % 2, :], w[:, c, f0:f0 + fw], hidT[:, c, 4 * b:4 * b + 4, :].rearrange("p r t -> p (r t)"), start=c == 0, stop=c == C - 1)
                    last.then_inc(s_smm, 1)
                    nf += 1
                pe.wait_ge(s_sact, nf)
                if b >= 1:
                    pe.wait_ge(s_sacc, b)
                for tb in range(TB):
                    for f, (f0, fw) in enumerate(FT):
                        last = nc.tensor.matmul(ps[:, 4 + tb // 2, (tb % 2) * D:(tb % 2 + 1) * D], sact3[0:fw, f, tb * P:(tb + 1) * P], swd[0:fw, f], start=f == 0, stop=f == 2)
                last.then_inc(s_sdn, 1)
                if b == 0:
                    pe.wait_ge(s_cnt, 1)
                    for h in range(2):
                        last = nc.tensor.matmul(ps[:, 6 + h, :], tri[:, h], rt[:, 9], start=True, stop=True)
                    last.then_inc(s_rank, 1)

            def expert(i, z, first):
                pe.wait_ge(s_xg[z], 16 * i + 16)
                units = [[(0, t, t) for t in range(4)], [(1, t, t) for t in range(4)], [(0, 4, 0), (1, 4, 1)]]
                for u, tiles in enumerate(units):
                    if not (first and u < 2):
                        pe.wait_ge(s_xev, 6 * i + 3 * z + u - 1)
                    for c, t, at in tiles:
                        last = nc.tensor.transpose(ps[:, 6 + (z + u) % 2, at * P:(at + 1) * P], xg[:, z, t, c * P:(c + 1) * P], ident[:])
                    last.then_inc(s_xtr, 1)
                pe.wait_ge(s_xev, 6 * i + 3 * z + 3)
                pe.wait_ge(s_ew[z], 48 * i + 48)
                for m in range(6):
                    hf, f = m // 3, m % 3
                    f0, fw = FT[f]
                    if not (first and m < 2):
                        pe.wait_ge(s_eact, 12 * i + 6 * z + m - 1)
                    for h, w in enumerate((ewg, ewu)):
                        for c in range(C):
                            last = nc.tensor.matmul(ps[0:fw, 2 * h + m % 2, 0:HALF], w[:, z, c, f0:f0 + fw], xgT[:, c, hf * HALF:(hf + 1) * HALF], start=c == 0, stop=c == C - 1)
                    last.then_inc(s_emm, 1)
                pe.wait_ge(s_eact, 12 * i + 6 * z + 6)
                for t in range(CT):
                    if not (first and t < 2):
                        pe.wait_ge(s_eev, 10 * i + 5 * z + t - 1)
                    for f, (f0, fw) in enumerate(FT):
                        last = nc.tensor.matmul(ps[:, 4 + (z + t) % 2, 0:D], eact[0:fw, f, t * P:(t + 1) * P], ewd[0:fw, z, f], start=f == 0, stop=f == 2)
                    last.then_inc(s_edn, 1)
            expert(0, 0, True)
            expert(0, 1, False)
            with pe.Fori(1, NE // 2) as i:
                for z in range(2):
                    expert(i, z, False)

        @block.scalar
        def _(act):
            act.preload_act_table(ACT.Tanh)
            act.wait_ge(s_const, LOADED)
            nc.scalar.activation(a_bc[:], a_bc[:], ACT.Exp).then_inc(s_dtm, 1)
            nc.scalar.activation(a_q[:], a_q[:], ACT.Exp).then_inc(s_dtm, 1)
            nc.scalar.activation(dt_bc[:], dt_bc[:], ACT.Exp).then_inc(s_dtm, 1)
            nc.scalar.activation(dt_q[:], dt_q[:], ACT.Exp).then_inc(s_dtm, 1)
            act.wait_ge(s_dta, 1)
            nc.scalar.activation(lam[:], dta_q[:], ACT.Exp, scale=-float(P)).then_inc(s_lam, 1)
            def steps(i, kernel):
                for n in range(2 * G):
                    act.wait_ge(s_zt, 2 * G * i + n + 1)
                    nc.scalar.activation(hring[:, n], zt[:, n % 2].rearrange("p (k q) -> p k q", k=C)[:, :, 0:B], ACT.Tanh).then_inc(s_h, 1)
                    if kernel and 2 <= n < 2 + CG * NH:
                        if n == 2:
                            act.wait_ge(s_kq, i + 1)
                        last = nc.scalar.activation(qx[:, 0, n - 2], qx[:, 0, n - 2], ACT.Exp, scale=-1.0)
                        if n == 1 + CG * NH:
                            last.then_inc(s_kqe, 1)
            with act.Fori(0, NCH) as i:
                steps(i, True)
            with act.Fori(NCH, S // G // 2) as i:
                steps(i, False)

            def powers(s, z):
                act.wait_ge(s_pa, s + 1)
                nc.scalar.activation(tp[:, z, :, :, P:P + NST], tp[:, z, :, :, P:P + NST], ACT.Exp, scale=consts[:, 4:5]).then_inc(s_pe, 1)

            def decays(s, z):
                act.wait_ge(s_qa, s + 1)
                nc.scalar.activation(qx[:, z], qx[:, z], ACT.Exp, scale=-1.0).then_inc(s_qe, 1)

            def sums_out(s, z, wait):
                if wait:
                    act.wait_ge(s_ytr, s - 1)
                for hb in range(2):
                    act.wait_ge(s_qmm, 2 * s + hb + 1)
                    nc.scalar.activation(ysb[:, z, 2 * hb:2 * hb + 2], ps[:, 2 * z + hb, 0:2 * (P + NST)].rearrange("p (g t) -> p g t", g=2)[:, :, 0:P], ACT.Copy).then_inc(s_y, 1)
            for z in range(2):
                powers(z, z)
                decays(z, z)
            for s in range(2):
                sums_out(s, s, False)
                powers(s + 2, s)
                decays(s + 2, s)
            with act.Fori(1, NCH // 2 - 1) as i:
                for z in range(2):
                    sums_out(2 * i + z, z, True)
                    powers(2 * i + z + 2, z)
                    decays(2 * i + z + 2, z)
            for z in range(2):
                sums_out(NCH - 2 + z, z, True)
            act.preload_act_table(ACT.Sigmoid)

            def x1_out(b):
                for c in range(C):
                    act.wait_ge(s_zero, 1)
                    act.wait_ge(s_x1tr, 2 * b + c + 1)
                    nc.scalar.activation(x1T[:, c, bass.ds(TB * b, TB), :], ps[:, 6 + c, :].rearrange("p (r t) -> p r t", r=TB), ACT.Copy).then_inc(s_x1ev, 1)

            def gates(n, z, wait):
                act.wait_ge(s_gmm, n + 1)
                if wait:
                    act.wait_ge(s_new, n - 1)
                for q, function in enumerate((ACT.Sigmoid, ACT.Sigmoid, ACT.Identity)):
                    nc.scalar.activation(gbuf[:, z, q if q < 2 else 3], ps[:, 3 * z + q, :], function, bias=gb[:, q, z:z + 1]).then_inc(s_fic, 1)

            def hid_out(b):
                for c in range(C):
                    act.wait_ge(s_zero, 1)
                    act.wait_ge(s_htr, 2 * b + c + 1)
                    nc.scalar.activation(hid_tok[:, bass.ds(TB * b, TB), c * P:(c + 1) * P], ps[:, 6 + c, :].rearrange("p (r d) -> p r d", r=TB), ACT.Copy).then_inc(s_hev, 1)
            x1_out(0)
            x1_out(1)
            for z in range(2):
                gates(z, z, False)
            with act.Fori(1, B - 1) as b:
                x1_out(b + 1)
                for z in range(2):
                    gates(2 * b + z, z, True)
                hid_out(b - 1)
            for z in range(2):
                gates(2 * B - 2 + z, z, True)
            hid_out(B - 2)
            hid_out(B - 1)
            act.wait_ge(s_lg, 1)
            act.wait_ge(s_hid, 2 * B)
            nc.scalar.activation(lgT, ps[:, 0:2, :], ACT.Copy).then_inc(s_lge, 1)
            act.wait_ge(s_z, 1)
            nc.scalar.activation(rt[:, 1], rt[:, 1], ACT.Exp).then_inc(s_e, 1)
            act.preload_act_table(ACT.Silu)
            for nf in range(3 * B):
                fw = FT[nf % 3][1]
                act.wait_ge(s_smm, nf + 1)
                if nf >= 2:
                    act.wait_ge(s_sact, nf - 1)
                silu = nc.scalar.activation(ssil[0:fw, nf % 2], ps[0:fw, nf % 2, :], ACT.Silu)
                if nf < 3 * EARLY:
                    silu = nc.scalar.activation(sup[0:fw, nf % 2], ps[0:fw, 2 + nf % 2, :], ACT.Copy)
                silu.then_inc(s_ssil, 1)

            def expert(i, z, first):
                for m in range(6):
                    fw = FT[m % 3][1]
                    act.wait_ge(s_emm, 12 * i + 6 * z + m + 1)
                    if not (first and m < 2):
                        act.wait_ge(s_eact, 12 * i + 6 * z + m - 1)
                    nc.scalar.activation(esil[0:fw, m % 2], ps[0:fw, m % 2, 0:HALF], ACT.Silu).then_inc(s_esil, 1)
                for t in range(CT):
                    act.wait_ge(s_edn, 10 * i + 5 * z + t + 1)
                    if t == 0 and not first_two(i, z, first):
                        act.wait_ge(s_yst[z], 16 * i)
                    nc.scalar.activation(yo[:, z, t], ps[:, 4 + (z + t) % 2, 0:D], ACT.Copy).then_inc(s_eev, 1)

            def first_two(i, z, first):
                return isinstance(i, int) and i == 0
            expert(0, 0, True)
            expert(0, 1, False)
            with act.Fori(1, NE // 2) as i:
                for z in range(2):
                    expert(i, z, False)

        @block.vector
        def _(dve):
            chain = [0]

            def link(ins):
                ins.then_inc(s_c, 1)
                chain[0] = chain[0] + 1
                dve.wait_ge(s_c, chain[0])

            nc.vector.memset(ps[:, 0:4], 0.0).then_inc(s_ps0, 1)
            dve.wait_ge(s_const, LOADED)
            nc.vector.memset(xc[:], 0.0)
            nc.vector.tensor_copy(hring[:, 2 * G - 1], h0r[:]).then_inc(s_h, 1)
            dve.wait_ge(s_dtm, 4)
            nc.vector.tensor_tensor(dta_q[:], dt_q[:].unsqueeze(2).to_broadcast([P, NG, NH]), a_q[:].unsqueeze(1).to_broadcast([P, NG, NH]), ALU.mult).then_inc(s_dta, 1)

            def kernel_states(i):
                c = c_q[:, bass.ds(CG * i, CG), :].rearrange("p g h -> p (g h)")
                nc.vector.tensor_tensor(cblk.rearrange("p g h j -> p (g h) j"), c.unsqueeze(2).to_broadcast([P, CG * NH, J]), consts[:, 0:J].unsqueeze(1).to_broadcast([P, CG * NH, J]), ALU.mult).then_inc(s_kc, 1)

            def kernel_out(i):
                dve.wait_ge(s_kmm, i + 1)
                dve.wait_ge(s_kst, 16 * CG * i + 16)
                nc.vector.tensor_scalar(ksb[:, 1:P], ps[:, 2, 1:P], 1.0, None, ALU.mult)
                nc.vector.tensor_tensor(ksb[:, 0:1], ps[:, 2, 0:1], d_k[:, bass.ds(i, 1)], ALU.add).then_inc(s_kev, 1)

            IT = S // G // 2

            def keep(i, half):
                dve.wait_ge(s_h, 2 * G * i + G * half + G + 1)
                nc.vector.tensor_scalar(uT[:, :, bass.ds(i * (-2 * G) + (S - G - G * half), G), :], hring[:, G * half:G * half + G][:, ::-1].rearrange("p t k b -> p k t b"), 1.0, None, ALU.mult).then_inc(s_hist, 1)

            def turn(i, n):
                dve.wait_ge(s_sum, 2 * G * i + n + 1)
                bank, t = n // G, n % G
                nc.vector.transpose(zt[:, n % 2], ps[:, bank, t * W:(t + 1) * W]).then_inc(s_zt, 1)
            def steps(i, kernel):
                for n in range(2 * G):
                    turn(i, n)
                    if n == G:
                        keep(i, 0)
                    if kernel and n == 4:
                        kernel_states(i)
                    if kernel and n == 13:
                        kernel_out(i)
                keep(i, 1)
            with dve.Fori(0, NCH) as i:
                steps(i, True)
            with dve.Fori(NCH, IT) as i:
                steps(i, False)
            n = 0
            for tb in range(TB):
                for k in range(C):
                    for bq in range(2):
                        dve.wait_ge(s_utr, n + 1)
                        for j in range(J):
                            last = nc.vector.tensor_copy(u_tok[:, Q * k:Q * k + Q, j, :].rearrange("p g (b t) -> p g b t", t=TB)[:, :, 4 * bq:4 * bq + 4, tb],
                                                         ps[:, 2 + n % 4, :].rearrange("p (b j g) -> p j g b", b=4, j=J)[:, j])
                        last.then_inc(s_uev, 1)
                        n += 1

            def states(z, chunk):
                nc.vector.tensor_scalar(ust[:, z].rearrange("p g j r -> p (g j r)"), u_tok[:, bass.ds(CG * chunk, CG)].rearrange("p g j r -> p (g j r)"), 1.0, None, ALU.mult).then_inc(s_ust, 1)

            def carry(chunk, z):
                dve.wait_ge(s_tmm, chunk + 1)
                for hb in range(2):
                    last = nc.vector.transpose(stt[:, z].rearrange("p (hb gn) r -> p hb (gn r)", hb=2)[:, hb].rearrange("p (g n) -> p g n", g=2),
                                               ps[:, 2 * z + hb, 0:2 * (P + NST)].rearrange("p (g t) -> p g t", g=2)[:, :, P:P + NST])
                link(last)
                sv = stt[:, z].rearrange("p n (b t) -> p n b t", t=TB)
                lv = lam[:, bass.ds(CG * chunk, CG), :].rearrange("p g h -> p (g h)").unsqueeze(2).to_broadcast([P, CG * NH, B])
                for tb in range(1, TB - 1):
                    link(nc.vector.tensor_tensor(ctmp, sv[:, :, :, tb - 1], lv, ALU.mult))
                    link(nc.vector.tensor_tensor(sv[:, :, :, tb], sv[:, :, :, tb], ctmp, ALU.add))
                cv = c_q[:, bass.ds(CG * chunk, CG), :].rearrange("p g h -> p (g h)").unsqueeze(2).unsqueeze(3).to_broadcast([P, CG * NH, B, TB - 1])
                nc.vector.tensor_tensor(xc[:, z].rearrange("p n (b t) -> p n b t", t=TB)[:, :, :, 1:TB], sv[:, :, :, 0:TB - 1], cv, ALU.mult).then_inc(s_xc, 1)

            def add_x(chunk, z):
                dve.wait_ge(s_ytr, chunk + 1)
                for j in range(J):
                    xv = xtok[:, :, bass.ds(NG * j + CG * chunk, CG)].rearrange("p r g -> p g r")
                    last = nc.vector.tensor_tensor(xv, ps[:, 4 + z, :].rearrange("p (g j r) -> p j g r", g=CG, j=J)[:, j], xv, ALU.add)
                last.then_inc(s_x1, 1)
            dve.wait_ge(s_uev, 16)
            dve.wait_ge(s_x, 16)
            PER = 5
            base = chain[0]
            for z in range(2):
                states(z, z)
            for s in range(2):
                carry(s, s)
                states(s, s + 2)
            assert chain[0] == base + 2 * PER
            with dve.Fori(1, NCH // 2 - 1) as i:
                chain[0] = i * (2 * PER) + base
                for z in range(2):
                    carry(2 * i + z, z)
                    states(z, 2 * i + z + 2)
                    add_x(2 * i + z - 2, z)
            chain[0] = base + PER * (NCH - 2)
            for z in range(2):
                carry(NCH - 2 + z, z)
                add_x(NCH - 4 + z, z)
            for z in range(2):
                add_x(NCH - 2 + z, z)
            zeros = zero[:, 0:512]

            def sums(n, z):
                dve.wait_ge(s_w, n + 1)
                nc.vector.tensor_tensor_scan(gbuf[:, z, 7], gbuf[:, z, 5], zeros, 0.0, ALU.add, ALU.add).then_inc(s_cs, 1)

            def gate(n, b, z, first):
                v = lambda m: gbuf[:, z, m]
                dve.wait_ge(s_fic, 3 * n + 2)
                link(nc.vector.scalar_tensor_tensor(v(2), v(0), EPS, v(1), ALU.add, ALU.add))
                nc.vector.reciprocal(v(2), v(2)).then_inc(s_r, 1)
                if not first:
                    sums(n - 1, 1 - z)
                dve.wait_ge(s_ap, n + 1)
                link(nc.vector.tensor_scalar(v(4), v(4), EPS, None, ALU.add))
                nc.vector.tensor_tensor_scan(v(7)[:, ::-1], v(4)[:, ::-1], zeros, 1.0, ALU.mult, ALU.add).then_inc(s_q, 1)
                nc.vector.tensor_tensor_scan(v(6), v(4), zeros, h0g[:, z, bass.ds(b, 1)], ALU.mult, ALU.add)
            base = chain[0]
            for z in range(2):
                gate(z, 0, z, z == 0)
            with dve.Fori(1, B) as b:
                chain[0] = b * 4 + base
                for z in range(2):
                    gate(2 * b + z, b, z, False)
            chain[0] = base + 4 * B
            sums(2 * B - 1, 1)
            def shared_sum(b):
                dve.wait_ge(s_sdn, b + 1)
                dve.wait_ge(s_hadd, 2 * b + 2)
                for q in range(2):
                    last = nc.vector.tensor_tensor(xtok[:, 4 * b + 2 * q:4 * b + 2 * q + 2, :], ps[:, 4 + q, :].rearrange("p (r d) -> p r d", r=2), xtok[:, 4 * b + 2 * q:4 * b + 2 * q + 2, :], ALU.add)
                last.then_inc(s_sacc, 1)

            v = lambda m: rt[:, m].rearrange("p (r e) -> p r e", e=NE)
            row = lambda m: sm[:, m]
            wide = lambda m: sm[:, m].unsqueeze(2).to_broadcast([P, R, NE])
            each = lambda a: a.unsqueeze(1).to_broadcast([P, R, NE])
            dve.wait_ge(s_ltr, 1)
            for q in range(2):
                for tb in range(TB):
                    last = nc.vector.tensor_tensor(v(0).rearrange("p (b t) e -> p b t e", t=TB)[:, J * q:J * q + J, tb], ps[:, 6 + q, tb * P:(tb + 1) * P].rearrange("p (j e) -> p j e", j=J)[:, :, 0:NE],
                                                   rb[:].unsqueeze(1).to_broadcast([P, J, NE]), ALU.add)
            link(last)
            link(nc.vector.tensor_reduce(row(0), v(0), AX.X, ALU.max))
            nc.vector.tensor_tensor(v(1), v(0), wide(0), ALU.subtract).then_inc(s_z, 1)
            dve.wait_ge(s_e, 1)
            link(nc.vector.tensor_reduce(row(1), v(1), AX.X, ALU.add))
            link(nc.vector.reciprocal(row(2), row(1)))
            link(nc.vector.tensor_tensor(v(2), v(1), wide(2), ALU.mult))
            for k in range(K):
                p, val, at, eq, oh = 2 + 4 * k, 3 + k, 5 + k, 3, 4 + k
                if k == 1:
                    link(nc.vector.scalar_tensor_tensor(v(p), v(4), -4.0, v(2), ALU.mult, ALU.add))
                link(nc.vector.tensor_reduce(row(val), v(p), AX.X, ALU.max))
                link(nc.vector.tensor_tensor(v(eq), v(p), wide(val), ALU.is_equal))
                link(nc.vector.scalar_tensor_tensor(v(eq), v(eq), -float(NE), each(iota_e[:, 0]), ALU.mult, ALU.add))
                link(nc.vector.tensor_reduce(row(at), v(eq), AX.X, ALU.min))
                link(nc.vector.tensor_tensor(v(oh), each(iota_e[:, 1]), wide(at), ALU.is_equal))
            nc.vector.tensor_tensor(v(9), v(4), v(5), ALU.add).then_inc(s_cnt, 1)
            shared_sum(0)
            dve.wait_ge(s_rank, 1)
            by_e = lambda m: rt[:, m].rearrange("p (e r) -> p e r", r=R)
            link(nc.vector.tensor_copy(by_e(7), ps[:, 7, :].rearrange("p (r e) -> p e r", e=NE)))
            link(nc.vector.tensor_tensor_scan(rt[:, 8], resets[:].rearrange("p e r -> p (e r)"), rt[:, 7], 0.0, ALU.mult, ALU.add))
            link(nc.vector.tensor_tensor(rt[:, 8], rt[:, 8], rt[:, 7], ALU.subtract))
            link(nc.vector.tensor_tensor(v(3), ps[:, 6, :].rearrange("p (r e) -> p r e", e=NE), by_e(8).rearrange("p e r -> p r e"), ALU.add))
            for k in range(K):
                link(nc.vector.tensor_tensor(v(10 + k), v(4 + k), v(3), ALU.mult))
                link(nc.vector.tensor_reduce(row(7 + k), v(10 + k), AX.X, ALU.add))
                link(nc.vector.tensor_scalar(row(9), row(7 + k), float(CAP), None, ALU.is_lt))
                nc.vector.tensor_scalar(row(10), row(7 + k), float(CAP - 1), float(NE * CAP), ALU.min, ALU.add)
                link(nc.vector.tensor_tensor(row(11 + k), row(3), row(4), ALU.add))
                link(nc.vector.tensor_scalar(row(11 + k), row(11 + k), 1e-9, None, ALU.add))
                link(nc.vector.reciprocal(row(11 + k), row(11 + k)))
                link(nc.vector.tensor_tensor(row(11 + k), row(11 + k), row(3 + k), ALU.mult))
                link(nc.vector.tensor_tensor(wt[:, k], row(11 + k), row(9), ALU.mult))
                link(nc.vector.scalar_tensor_tensor(row(13), row(5 + k), float(CAP), row(10), ALU.mult, ALU.add))
                nc.vector.tensor_copy(idx[:, 2 + k], row(13))
                link(nc.vector.tensor_scalar(row(14), row(9), -float(2 * NE * CAP), float(2 * NE * CAP), ALU.mult, ALU.add))
                link(nc.vector.tensor_tensor(row(15), row(14), row(13), ALU.add))
                last = nc.vector.tensor_copy(idx[:, k], row(15))
            last.then_inc(s_idx, 1)

            for b in range(1, B):
                if b >= EARLY:
                    for f, (f0, fw) in enumerate(FT):
                        nf = 3 * b + f
                        dve.wait_ge(s_ssil, nf + 1)
                        dve.wait_ge(s_sdn, b)
                        nc.vector.tensor_tensor(sact3[0:fw, f], ssil[0:fw, nf % 2], ps[0:fw, 2 + nf % 2, :], ALU.mult).then_inc(s_sact, 1)
                shared_sum(b)

            def expert(i, z, first):
                for u in range(3):
                    dve.wait_ge(s_xtr, 6 * i + 3 * z + u + 1)
                    if u == 0 and not first:
                        dve.wait_ge(s_emm, 12 * i + 6 * z)
                    pv = ps[:, 6 + (z + u) % 2]
                    if u < 2:
                        ins = nc.vector.tensor_copy(xgT[:, u, 0:4 * P], pv)
                    else:
                        ins = nc.vector.tensor_copy(xgT[:, :, 4 * P:5 * P], pv[:, 0:2 * P].rearrange("p (c t) -> p c t", c=C))
                    ins.then_inc(s_xev, 1)
                for m in range(6):
                    hf, f = m // 3, m % 3
                    fw = FT[f][1]
                    dve.wait_ge(s_esil, 12 * i + 6 * z + m + 1)
                    if m == 0 and not first:
                        dve.wait_ge(s_edn, 10 * i + 5 * z)
                    nc.vector.tensor_tensor(eact[0:fw, f, hf * HALF:(hf + 1) * HALF], esil[0:fw, m % 2], ps[0:fw, 2 + m % 2, 0:HALF], ALU.mult).then_inc(s_eact, 1)
            expert(0, 0, True)
            expert(0, 1, False)
            with dve.Fori(1, NE // 2) as i:
                for z in range(2):
                    expert(i, z, False)
            for n in range(K * R):
                r, k = n // 2, n % 2
                dve.wait_ge(s_g[n % NGB], 16 * (n // NGB) + 16)
                if k == 1:
                    dve.wait_ge(s_comb, n)
                nc.vector.scalar_tensor_tensor(xtok[:, r], gath[:, n % NGB], wt[:, k, r:r + 1], xtok[:, r], ALU.mult, ALU.add).then_inc(s_comb, 1)




def kernel(x, cond_1024, L0_cond_Wx, L0_cond_Wh, L0_cond_b, L0_attn_A_log, L0_attn_D, L0_attn_C_re, L0_attn_C_im,
           L0_attn_log_dt, L0_cond2_W_f, L0_cond2_b_f, L0_cond2_W_i, L0_cond2_b_i, L0_cond2_W_h, L0_cond2_b_h,
           L0_ffn_router_w, L0_ffn_router_b, L0_ffn_w_gate, L0_ffn_w_up, L0_ffn_w_down, L0_ffn_sw_gate,
           L0_ffn_sw_up, L0_ffn_sw_down):
    import numpy as np
    import concourse.bacc as bacc
    from concourse.bass_utils import run_bass_kernel_spmd

    f32 = np.float32

    def rows(w):
        return np.asarray(w).reshape(C, P, -1).transpose(1, 0, 2)

    def rec(w):
        return np.asarray(w).reshape(J, C, Q, -1).transpose(0, 2, 1, 3).reshape(P, C, -1)

    def down(w):
        w = np.asarray(w)
        w = np.concatenate([w, np.zeros((3 * P - F, D), f32)])
        return w.reshape(3, P, D).transpose(1, 0, 2)

    x = np.asarray(x)
    cond = np.asarray(cond_1024)
    a_log, c_re, dt = np.asarray(L0_attn_A_log), np.asarray(L0_attn_C_re), np.asarray(L0_attn_log_dt)
    d_k = np.zeros((J, Q, NCH), f32)
    d_k[:, :J] = np.asarray(L0_attn_D).reshape(J, NCH, CG).transpose(2, 0, 1)
    consts = np.zeros((P, 8), f32)
    consts[np.arange(P), np.arange(P) // Q] = 1
    consts[:, 4] = -(np.arange(P) + 1)
    resets = np.ones((P, NE, R), f32)
    resets[:, :, 0] = 0
    iota_e = np.stack([np.arange(NE), np.arange(NE) - NE]).astype(f32)
    tri = np.stack([np.triu(np.ones((P, P)), 1), np.ones((P, P))], 1).astype(f32)
    arrays = {
        "x_tok": x.reshape(B, TB, P, D).transpose(2, 0, 1, 3).reshape(P, R, D),
        "x_steps": x.reshape(B, S // G, G, C, P).transpose(1, 4, 3, 2, 0),
        "h0_rec": rec(cond.T),
        "h0_gate": rows(cond.T),
        "wx": rows(L0_cond_Wx),
        "wh": rec(L0_cond_Wh),
        "b_rec": np.asarray(L0_cond_b)[None],
        "a_bc": np.broadcast_to(a_log, (P, NST)),
        "a_q": np.tile(a_log.reshape(NH, Q).T, (J, 1)),
        "dt_bc": np.broadcast_to(dt.reshape(J, NG).T, (P, NG, J)),
        "dt_q": np.repeat(dt.reshape(J, NG), Q, 0),
        "c_q": c_re.reshape(J, NG, NH, Q).transpose(0, 3, 1, 2).reshape(P, NG, NH),
        "d_k": d_k.reshape(P, NCH),
        "gate_w": np.stack([rows(np.asarray(w).T) for w in (L0_cond2_W_f, L0_cond2_W_i, L0_cond2_W_h)], 1),
        "gate_b": np.stack([np.asarray(v).reshape(C, P).T for v in (L0_cond2_b_f, L0_cond2_b_i, L0_cond2_b_h)], 1),
        "router_w": rows(L0_ffn_router_w),
        "router_b": np.broadcast_to(np.asarray(L0_ffn_router_b), (P, NE)),
        "sh_gate": rows(L0_ffn_sw_gate),
        "sh_up": rows(L0_ffn_sw_up),
        "sh_down": down(L0_ffn_sw_down),
        "ex_gate": np.stack([rows(w) for w in np.asarray(L0_ffn_w_gate)]),
        "ex_up": np.stack([rows(w) for w in np.asarray(L0_ffn_w_up)]),
        "ex_down": np.stack([down(w) for w in np.asarray(L0_ffn_w_down)]),
        "ident": np.eye(P, dtype=f32),
        "consts": consts,
        "iota_t": np.broadcast_to(np.arange(P, dtype=f32), (P, P)),
        "tri": tri,
        "resets": resets,
        "iota_e": np.broadcast_to(iota_e, (P, 2, NE)),
    }
    arrays = {"in_" + n: np.ascontiguousarray(a) for n, a in arrays.items()}
    nc = bacc.Bacc("TRN2", target_bir_lowering=False, num_devices=1)
    args = [nc.dram_tensor(n, a.shape, mybir.dt.from_np(a.dtype), kind="ExternalInput").ap() for n, a in arrays.items()]
    out = nc.dram_tensor("out", [P, R, D], F32, kind="ExternalOutput").ap()
    build(nc, *args, out)
    got = run_bass_kernel_spmd(nc, [arrays], core_ids=[0]).results[0]["out"]
    return got.reshape(P, B, TB, D).transpose(1, 2, 0, 3).reshape(B, S, D)
```

```python
from contextlib import ExitStack

import concourse.bass as bass
from concourse import mybir

F32 = mybir.dt.float32
I32 = mybir.dt.int32
BF16 = mybir.dt.bfloat16
F32R = mybir.dt.float32r
ACT = mybir.ActivationFunctionType
ALU = mybir.AluOpType
AX = mybir.AxisListType

P = 128
B, S, D = 8, 512, 256
C = D // P
TB = S // P
R = B * TB
Q = 32
J = P // Q
W = D // J
FILL = 256
G = 8
NST = 64
NH = NST // Q
NG = D // J
CG = 4
NCH = NG // CG
F = 352
FT = [(0, 128), (128, 128), (256, 96)]
NE, K = 16, 2
CAP = int(-(-1.25 * B * S * K // NE))
CT = CAP // P
HALF = CAP // 2
DX = D + 1
XG = 2 * CT * DX
EW = 2 * C * F + 3 * D
N = B * S
NOWHERE = 2 * K * N
PIECES = 8
BACK = 4
EPS = 1e-8
WARM = 8
TURNS = [[(0, t, 6, t) for t in range(4)], [(1, t, 7, t) for t in range(4)], [(c, 4, 6, c) for c in range(2)]]
HADD = 3
EARLY = 2


def build(nc, x_tok, x_steps, h0_rec, h0_gate, wx_d, wh_d, b_rec_d, a_bc_d, a_q_d, dt_bc_d, dt_q_d, c_q_d, d_k_d,
          gate_w, gate_b, router_w, router_b, sh_gate, sh_up, sh_down, ex_gate, ex_up, ex_down,
          ident_d, consts_d, iota_t_d, tri_d, resets_d, iota_e_d, rows_to_d, out):
    k_pad = nc.dram_tensor("k_pad", [D, 2 * P], F32).ap()
    slots_in = nc.dram_tensor("slots_in", [NE * CAP, DX], F32).ap()
    results = nc.dram_tensor("results", [K * N, D], F32).ap()

    with ExitStack() as ctx:
        def sb(name, shape, dt=F32):
            return ctx.enter_context(nc.sbuf_tensor(name, shape, dt))

        def sem(name):
            return ctx.enter_context(nc.semaphore(name))

        xtok = sb("xtok", [P, R, D])
        brow = sb("brow", [1, D])
        h0r = sb("h0r", [P, C, B])
        h0g = sb("h0g", [P, C, B])
        a_bc = sb("a_bc", [P, NST])
        a_q = sb("a_q", [P, NH])
        dt_bc = sb("dt_bc", [P, NG, J])
        dt_q = sb("dt_q", [P, NG])
        c_q = sb("c_q", [P, NG, NH])
        d_k = sb("d_k", [P, NCH])
        dta_q = sb("dta_q", [P, NG, NH])
        lam = sb("lam", [P, NG, NH])
        gb = sb("gb", [P, 3, C])
        rw = sb("rw", [P, C, NE])
        rb = sb("rb", [P, NE])
        ident = sb("ident", [P, P])
        consts = sb("consts", [P, 8])
        iota_t = sb("iota_t", [P, P])
        tri = sb("tri", [P, 2, P])
        resets = sb("resets", [P, NE, R])
        iota_e = sb("iota_e", [P, 2, NE])
        zero = sb("zero", [P, 512])
        sw_hi = sb("sw_hi", [P, EW], F32R)
        rows_to = sb("rows_to", [P, K, R])
        dest = sb("dest", [P, 2, CT], I32)

        xst = sb("xst", [P, 2, C, G, B])
        zt = sb("zt", [P, 2, W])
        hring = sb("hring", [P, 2 * G, C, B])

        shared = ExitStack()
        wx = shared.enter_context(nc.sbuf_tensor("wx", [P, C, D], F32))
        wh = shared.enter_context(nc.sbuf_tensor("wh", [P, C, D], F32))
        gw = shared.enter_context(nc.sbuf_tensor("gw", [P, 3, C, D], F32))
        big = shared.enter_context(nc.sbuf_tensor("big", [P, R * D], F32))
        uT = big[:, :].rearrange("p (k t b) -> p k t b", k=C, b=B)
        hidT = big[:, :].rearrange("p (c r t) -> p c r t", c=C, t=P)
        tok = shared.enter_context(nc.sbuf_tensor("tok", [P, R * DX], F32))
        u_tok = tok[:, 0:R * D].rearrange("p (g j r) -> p g j r", j=J, r=R)
        hid_tok = tok[:, :].rearrange("p (r d) -> p r d", d=DX)
        mid = shared.enter_context(nc.sbuf_tensor("mid", [P, R * D], F32))
        x1T = mid[:, :].rearrange("p (c r t) -> p c r t", c=C, t=P)
        blank = mid[:, 0:CT * DX].rearrange("p (t d) -> p t d", t=CT)
        arena = shared.enter_context(nc.sbuf_tensor("arena", [P, 11776], F32))

        def part(at, shape):
            n = 1
            for s in shape:
                n *= s
            v = arena[:, at:at + n]
            if len(shape) == 2:
                return v.rearrange("p (a b) -> p a b", a=shape[0])
            if len(shape) == 3:
                return v.rearrange("p (a b c) -> p a b c", a=shape[0], b=shape[1])
            if len(shape) == 4:
                return v.rearrange("p (a b c d) -> p a b c d", a=shape[0], b=shape[1], c=shape[2])
            return v

        tp = part(0, [2, CG, J, P + NST])
        qx = part(6144, [2, CG * NH, P])
        ust = part(8192, [2, CG, J, R])
        stt = part(9216, [2, CG * NH, R])
        xc = part(9728, [2, CG * NH, R])
        ysb = part(10240, [2, CG, P])
        ctmp = part(11264, [CG * NH, B])
        cblk = part(11328, [CG, NH, J])
        ksb = part(11392, [P])
        gbuf = part(0, [2, 8, 512])
        rt = part(0, [14, R * NE])
        sm = part(7168, [16, R])
        idx = arena[:, 7680:7680 + 4 * R].bitcast(I32).rearrange("p (k r) -> p k r", k=4)
        wt = part(7808, [2, R])
        lgT = part(8000, [2, 512])
        sw = part(9100, [EW])
        sact3 = mid[:, 6416:7952].rearrange("p (f t) -> p f t", f=3)
        ssil = part(8000, [2, 512])
        early_sil = mid[:, 0:1536].rearrange("p (z t) -> p z t", z=3)
        early_up = mid[:, 2576:4112].rearrange("p (z t) -> p z t", z=3)
        xg = mid[:, 0:XG].rearrange("p (z t d) -> p z t d", z=2, t=CT)
        esil = mid[:, 5136:5776].rearrange("p (z t) -> p z t", z=2)
        eprod = mid[:, 5776:6416].rearrange("p (z t) -> p z t", z=2)
        yo = arena[:, 0:2560].rearrange("p (z t d) -> p z t d", z=2, t=CT)
        ew = arena[:, 2560:2560 + 2 * EW].rearrange("p (z w) -> p z w", z=2)
        back = (big[:, :].rearrange("p (r d) -> p r d", d=D), tok[:, 0:R * D].rearrange("p (r d) -> p r d", d=D))
        shared.close()
        taken = ExitStack()

        def place(name, shape, dt=F32R):
            return taken.enter_context(nc.sbuf_tensor(name, shape, dt))
        OLD = 5 * C * D
        sw_lo = place("sw_lo", [P, EW])
        place("weights_rest", [P, OLD - EW + R * D + R * DX + 2576], F32)
        sh_hi1 = place("sh_hi1", [P, C, 512])
        sh_lo1 = place("sh_lo1", [P, C, 512])
        sh_hi0 = place("sh_hi0", [P, C, 512])
        place("mid_gap", [P, 6416 - 2576 - 3 * C * 512], F32)
        sact_hi = place("sact_hi", [P, 3, 512])
        place("mid_end", [P, R * D - 6416 - 3 * 512], F32)
        sh_lo0 = place("sh_lo0", [P, C, 512])
        sact_lo = place("sact_lo", [P, 3, 512])
        sh_hi, sh_lo = (sh_hi0, sh_hi1), (sh_lo0, sh_lo1)
        taken.close()
        taken = ctx
        place("weights_old", [P, OLD], F32)
        eact_hi = place("eact_hi", [P, 3, CAP])
        eact_lo = place("eact_lo", [P, 3, CAP])
        ew_lo1 = place("ew_lo1", [P, EW])
        place("big_rest", [P, R * D - 6 * CAP - EW], F32)
        ew_hi = place("ew_hi", [P, 2, EW])
        ew_lo0 = place("ew_lo0", [P, EW])
        place("tok_rest", [P, R * DX - 3 * EW], F32)
        place("mid_front", [P, XG], F32)
        xgT_hi = place("xgT_hi", [P, C, CAP])
        xgT_lo = place("xgT_lo", [P, C, CAP])
        place("mid_rest", [P, R * D - XG - 2 * C * CAP], F32)
        place("arena_all", [P, 11776], F32)
        ew_lo = (ew_lo0, ew_lo1)
        gate_of = lambda w: w[:, 0:C * F].rearrange("p (c f) -> p c f", c=C)
        up_of = lambda w: w[:, C * F:2 * C * F].rearrange("p (c f) -> p c f", c=C)
        down_of = lambda w: w[:, 2 * C * F:EW].rearrange("p (f d) -> p f d", f=3)
        swg, swu, swd = gate_of(sw), up_of(sw), down_of(sw)

        ps = ctx.enter_context(nc.psum_tensor("ps", [P, 8, 512], F32))

        names = """s_first s_const s_x s_ps0 s_zero s_dtm s_dta s_lam s_kq s_kqe s_kc s_kmm s_kev s_sum s_zt s_h s_xdone s_hist
            s_utr s_uev s_uea s_ust s_pa s_pe s_qa s_qe s_tmm s_st s_xc s_qmm s_y s_ytr s_x1 s_c s_out
            s_x1tr s_x1ev s_gmm s_fic s_r s_ap s_ip s_new s_q s_w s_cs s_hid s_htr s_hev s_hadd s_hadd2 s_lg s_lge s_ltr s_z s_e s_cnt s_rank s_idx s_wt
            s_sw s_swhi s_swlo s_shhi s_shlo s_sahi s_salo s_smm s_ssil s_sact s_sdn s_sacc s_sc s_zf
            s_yz s_rows s_dest s_xtr s_xhi s_xev s_whi s_wlo s_emm s_esil s_eact s_ehi s_elo s_edn s_eev s_comb""".split()
        sems = {n: sem(n) for n in names}
        (s_first, s_const, s_x, s_ps0, s_zero, s_dtm, s_dta, s_lam, s_kq, s_kqe, s_kc, s_kmm, s_kev, s_sum, s_zt, s_h, s_xdone, s_hist,
         s_utr, s_uev, s_uea, s_ust, s_pa, s_pe, s_qa, s_qe, s_tmm, s_st, s_xc, s_qmm, s_y, s_ytr, s_x1, s_c, s_out,
         s_x1tr, s_x1ev, s_gmm, s_fic, s_r, s_ap, s_ip, s_new, s_q, s_w, s_cs, s_hid, s_htr, s_hev, s_hadd, s_hadd2, s_lg, s_lge, s_ltr, s_z, s_e, s_cnt, s_rank, s_idx, s_wt,
         s_sw, s_swhi, s_swlo, s_shhi, s_shlo, s_sahi, s_salo, s_smm, s_ssil, s_sact, s_sdn, s_sacc, s_sc, s_zf,
         s_yz, s_rows, s_dest, s_xtr, s_xhi, s_xev, s_whi, s_wlo, s_emm, s_esil, s_eact, s_ehi, s_elo, s_edn, s_eev, s_comb) = [sems[n] for n in names]
        s_xs = [sem("s_xs0"), sem("s_xs1")]
        s_kst = sem("s_kst")
        s_late = sem("s_late")
        s_t0 = [sem("s_t00"), sem("s_t01")]
        s_yst = [sem("s_yst0"), sem("s_yst1")]
        s_back = [sem(f"s_back{g}") for g in range(R // BACK)]
        s_ew = [sem("s_ew0"), sem("s_ew1")]
        s_xg = [sem("s_xg0"), sem("s_xg1")]
        block = ctx.enter_context(nc.Block())
        first = ((wx, wx_d), (tri, tri_d), (brow, b_rec_d), (wh, wh_d), (h0r, h0_rec))
        loads = ((a_q, a_q_d), (dt_q, dt_q_d), (a_bc, a_bc_d),
                 (dt_bc, dt_bc_d), (c_q, c_q_d), (d_k, d_k_d), (consts, consts_d), (iota_t, iota_t_d))
        late = ((ident, ident_d), (h0g, h0_gate), (gw, gate_w), (gb, gate_b), (rw, router_w), (rb, router_b),
                (resets, resets_d), (iota_e, iota_e_d), (rows_to, rows_to_d))
        FIRST_LOADED, LOADED, LATE = 16 * len(first), 16 * len(loads), 16 * len(late)

        def shared_banks(nf):
            pair = nf if nf < 2 else (nf + 1) % 2
            return pair, 2 + pair

        def sums_at(group, t):
            return ps[:, 2 * group + t % 2, t // 2 * W:(t // 2 + 1) * W]

        def u_out(engine, copy, half, done):
            for n in range(half, 2 * C * TB, 2):
                tb, k, bq = n // (2 * C), n // 2 % C, n % 2
                engine.wait_ge(s_utr, n + 1)
                for j in range(J):
                    last = copy(u_tok[:, Q * k:Q * k + Q, j, :].rearrange("p g (b t) -> p g b t", t=TB)[:, :, 4 * bq:4 * bq + 4, tb],
                                ps[:, 2 + n % 4, :].rearrange("p (b j g) -> p j g b", b=4, j=J)[:, j])
                last.then_inc(done, 1)

        @block.sync
        def _(sp):
            sp.dma_start(xst[:, 0], x_steps[0]).then_inc(s_xs[0], 16)
            for dst, src in first:
                sp.dma_start(dst[:], src).then_inc(s_first, 16)
            sp.dma_start(xst[:, 1], x_steps[1]).then_inc(s_xs[1], 16)
            for dst, src in loads:
                sp.dma_start(dst[:], src).then_inc(s_const, 16)
            sp.wait_ge(s_zero, 2)
            sp.dma_start(k_pad[:, 0:P].rearrange("(c p) t -> p c t", p=P), zero[:, 0:C * P].rearrange("p (c t) -> p c t", c=C)).then_inc(s_kst, 16)
            sp.wait_ge(s_kst, 16)
            kv = k_pad[:, P:2 * P].rearrange("(c q j) t -> j c q t", c=J, j=CG)

            def ahead(i, z):
                sp.wait_ge(s_xdone, 2 * i + z + 1)
                sp.dma_start(xst[:, z], x_steps[bass.ds(2 * i + 2 + z, 1)].rearrange("o p k t b -> (o p) k t b")).then_inc(s_xs[z], 16)
            with sp.Fori(0, NCH) as i:
                for z in range(2):
                    ahead(i, z)
                sp.wait_ge(s_kev, i + 1)
                for j in range(CG):
                    sp.dma_start(kv[j, :, bass.ds(i, 1)].rearrange("c q t -> (c q) t"), ksb[Q * j:Q * j + J]).then_inc(s_kst, 16)
                sp.dma_start(results[bass.ds(i * (K * N // NCH), K * N // NCH)].rearrange("(p t d) c -> p t (d c)", p=P, d=2), zero[:].unsqueeze(1).to_broadcast([P, K * N // NCH // P // 2, 2 * D])).then_inc(s_yz, 16)
            with sp.Fori(NCH, NCH + PIECES) as i:
                for z in range(2):
                    ahead(i, z)
                sp.dma_start(xtok[:, bass.ds(i * (R // PIECES) - NCH * (R // PIECES), R // PIECES)], x_tok[:, bass.ds(i * (R // PIECES) - NCH * (R // PIECES), R // PIECES)]).then_inc(s_x, 16)
                for e in range(NE // PIECES):
                    sp.dma_start(slots_in[bass.ds(i * (NE // PIECES * CAP) + (e * CAP - NCH * NE // PIECES * CAP), CAP)].rearrange("(p t) d -> p (t d)", p=P), blank.rearrange("p t d -> p (t d)")).then_inc(s_zf, 16)
            with sp.Fori(NCH + PIECES, S // G // 2 - 1) as i:
                for z in range(2):
                    ahead(i, z)
            for dst, src in late:
                sp.dma_start(dst[:], src).then_inc(s_late, 16)
            sp.wait_ge(s_kst, 16 + 16 * CG * NCH)
            kt = bass.AP(k_pad.tensor, 1, [[1, P], [2 * P * NG, J], [2 * P, NG], [1, P]])

            def toeplitz(z, chunk):
                for g in range(CG):
                    sp.dma_start(tp[:, z, g, :, 0:P], kt[:, :, bass.ds(chunk * CG + g, 1), :].rearrange("p j o t -> p j (o t)")).then_inc(s_t0[z], 16)
            for z in range(2):
                toeplitz(z, z)
            with sp.Fori(1, NCH // 2) as i:
                for z in range(2):
                    sp.wait_ge(s_tmm, 2 * i + z - 1)
                    toeplitz(z, 2 * i + z)
            sp.wait_ge(s_x1, NCH)
            sp.dma_start(swg, sh_gate).then_inc(s_sw, 16)
            sp.dma_start(swu, sh_up).then_inc(s_sw, 16)
            sp.dma_start(swd, sh_down).then_inc(s_sw, 16)

            def weights(z, e):
                sp.dma_start(gate_of(ew[:, z]), ex_gate[bass.ds(e, 1)].rearrange("o p c f -> (o p) c f")).then_inc(s_ew[z], 16)
                sp.dma_start(up_of(ew[:, z]), ex_up[bass.ds(e, 1)].rearrange("o p c f -> (o p) c f")).then_inc(s_ew[z], 16)
                sp.dma_start(down_of(ew[:, z]), ex_down[bass.ds(e, 1)].rearrange("o p c f -> (o p) c f")).then_inc(s_ew[z], 16)

            def inputs(z, e):
                sp.dma_start(xg[:, z], slots_in[bass.ds(e * CAP, CAP)].rearrange("(t p) d -> p t d", p=P)).then_inc(s_xg[z], 16)
            sp.wait_ge(s_idx, 1)
            for z in range(2):
                weights(z, z)
            sp.wait_ge(s_sc, 16 * R * K)
            for z in range(2):
                inputs(z, z)

            with sp.Fori(0, NE // 2 - 1) as i:
                for z in range(2):
                    sp.wait_ge(s_xtr, 6 * i + 3 * z + 3)
                    sp.wait_ge(s_dest, 2 * i + z + 1)
                    inputs(z, 2 * i + z + 2)
                    sp.wait_ge(s_wlo, 2 * i + z + 1)
                    weights(z, 2 * i + z + 2)
            for z in range(2):
                sp.wait_ge(s_yst[z], 8 * CT * NE)
            sp.wait_ge(s_edn, CT * NE)
            for g in range(R // BACK):
                for k in range(K):
                    sp.dma_start(back[k][:, BACK * g:BACK * g + BACK], results[k * N + g * BACK * P:k * N + (g + 1) * BACK * P].rearrange("(r p) d -> p r d", p=P)).then_inc(s_back[g], 16)
            for g in range(R // BACK):
                sp.wait_ge(s_comb, K * BACK * (g + 1))
                sp.dma_start(out[:, BACK * g:BACK * g + BACK], xtok[:, BACK * g:BACK * g + BACK]).then_inc(s_out, 16)
            sp.wait_ge(s_out, 16 * (R // BACK))

        @block.gpsimd
        def _(pool):
            pool.memset(zero[:], 0.0).then_inc(s_zero, 1)
            pool.memset(blank[:, :, 0:D], 0.0)
            pool.memset(blank[:, :, D:DX], float(NOWHERE)).then_inc(s_zero, 1)

            def decay_args(z, chunk, done):
                d = dta_q[:, bass.ds(CG * chunk, CG), :].rearrange("p g h -> p (g h)")
                pool.tensor_tensor(qx[:, z], d.unsqueeze(2).to_broadcast([P, CG * NH, P]), iota_t[:].unsqueeze(1).to_broadcast([P, CG * NH, P]), ALU.mult).then_inc(done, 1)

            def power_args(z, chunk):
                pool.tensor_tensor(tp[:, z, :, :, P:P + NST].rearrange("p g j n -> p (g j) n"), dt_bc[:, bass.ds(CG * chunk, CG), :].rearrange("p g j -> p (g j)").unsqueeze(2).to_broadcast([P, CG * J, NST]),
                                   a_bc[:].unsqueeze(1).to_broadcast([P, CG * J, NST]), ALU.mult).then_inc(s_pa, 1)
            pool.wait_ge(s_const, LOADED)
            pool.wait_ge(s_dta, 1)
            decay_args(0, 0, s_kq)

            zeros = zero[:, 0:C * G * B].rearrange("p (k t b) -> p k t b", k=C, b=B)

            def keep(i, half):
                group = hring[:, G * half:G * half + G][:, ::-1].rearrange("p t k b -> p k t b")
                pool.wait_ge(s_zero, 1)
                pool.wait_ge(s_h, 4 * G * i + 2 * G * half + 2 * G + 2)
                pool.tensor_tensor(uT[:, :, bass.ds(i * (-2 * G) + (S - G - G * half), G), :], group, zeros, ALU.add).then_inc(s_hist, 1)
            with pool.Fori(0, NCH - 1) as i:
                keep(i, 0)
                pool.wait_ge(s_zero, 1)
                pool.wait_ge(s_kmm, i + 1)
                decay_args(0, i + 1, s_kq)
                keep(i, 1)
            for half in range(2):
                keep(NCH - 1, half)
            pool.wait_ge(s_kmm, NCH)
            pool.wait_ge(s_dtm, 4)
            power_args(0, 0)
            power_args(1, 1)
            decay_args(0, 0, s_qa)
            decay_args(1, 1, s_qa)
            with pool.Fori(NCH, S // G // 2) as i:
                for half in range(2):
                    keep(i, half)

            def conv_args(s, z):
                pool.wait_ge(s_zero, 1)
                pool.wait_ge(s_tmm, s + 1)
                power_args(z, s + 2)
                pool.wait_ge(s_zero, 1)
                pool.wait_ge(s_qmm, 2 * s + 2)
                decay_args(z, s + 2, s_qa)
            with pool.Fori(0, NCH // 2 - 1) as i:
                for z in range(2):
                    conv_args(2 * i + z, z)
            def gate_products(n, b, z):
                v = lambda m: gbuf[:, z, m]
                started = not isinstance(n, int)
                pool.wait_ge(s_zero, 1)
                pool.wait_ge(s_r, n + 1)
                pool.tensor_tensor(v(4), v(0), v(2), ALU.mult).then_inc(s_ap, 1)
                if started:
                    pool.wait_ge(s_zero, 1)
                    pool.wait_ge(s_cs, n - 1)
                pool.tensor_tensor(v(5), v(1), v(2), ALU.mult).then_inc(s_ip, 1)
                pool.wait_ge(s_zero, 1)
                pool.wait_ge(s_ip, n + 1)
                pool.wait_ge(s_fic, 3 * n + 3)
                pool.tensor_tensor(v(5), v(5), v(3), ALU.mult).then_inc(s_new, 1)
                if started:
                    hidden_sum(n - 2, b - 1, z)
                if started or n == 1:
                    scaled_new(n - 1, 1 - z)

            def scaled_new(n, z):
                pool.wait_ge(s_zero, 1)
                pool.wait_ge(s_q, n + 1)
                pool.wait_ge(s_new, n + 1)
                pool.tensor_tensor(gbuf[:, z, 5], gbuf[:, z, 5], gbuf[:, z, 7], ALU.mult).then_inc(s_w, 1)

            def hidden_sum(n, b, z):
                pool.wait_ge(s_zero, 1)
                pool.wait_ge(s_cs, n + 1)
                pool.tensor_tensor(hidT[:, z, bass.ds(TB * b, TB), :].rearrange("p r t -> p (r t)"), gbuf[:, z, 7], gbuf[:, z, 6], ALU.add).then_inc(s_hid, 1)
            for z in range(2):
                gate_products(z, 0, z)
            with pool.Fori(1, B) as b:
                for z in range(2):
                    gate_products(2 * b + z, b, z)
            hidden_sum(2 * B - 2, B - 1, 0)
            scaled_new(2 * B - 1, 1)
            hidden_sum(2 * B - 1, B - 1, 1)
            def add_hidden(b):
                for c in range(C):
                    pool.wait_ge(s_hev, 2 * b + c + 1)
                    pool.tensor_tensor(xtok[:, 4 * b:4 * b + 4, c * P:(c + 1) * P], xtok[:, 4 * b:4 * b + 4, c * P:(c + 1) * P],
                                       hid_tok[:, 4 * b:4 * b + 4, c * P:(c + 1) * P], ALU.add).then_inc(s_hadd, 1)

            def early_products(b):
                for f, (f0, fw) in enumerate(FT):
                    pool.wait_ge(s_ssil, 3 * b + f + 1)
                    if b >= 1:
                        pool.wait_ge(s_sdn, b)
                    pool.tensor_tensor(sact3[0:fw, f], early_sil[0:fw, f], early_up[0:fw, f], ALU.mult).then_inc(s_sact, 1)
            early_products(0)
            add_hidden(0)
            pool.wait_ge(s_swhi, 1)
            pool.wait_ge(s_gmm, 2 * B)
            pool.tensor_tensor(sw_lo[:], sw, sw_hi[:].bitcast(F32), ALU.subtract).then_inc(s_swlo, 1)
            early_products(1)
            for b in range(1, HADD):
                add_hidden(b)
            pool.wait_ge(s_zf, 16 * NE)
            pool.wait_ge(s_idx, 1)
            pool.wait_ge(s_late, LATE)
            for k in range(K):
                if k >= 1:
                    pool.wait_ge(s_sc, 16 * R * k)
                pool.tensor_copy(hid_tok[:, :, D], rows_to[:, k]).then_inc(s_rows, 1)
                pool.wait_ge(s_rows, k + 1)
                for r in range(R):
                    pool.indirect_dma_start(out=slots_in[:, :], out_offset=bass.IndirectOffsetOnAxis(ap=idx[:, k, r:r + 1], axis=0),
                                            in_=hid_tok[:, r, :], in_offset=None, bounds_check=NE * CAP - 1, oob_is_err=False).then_inc(s_sc, 16)

            def weights_lo(i, z, wait):
                pool.wait_ge(s_zero, 1)
                pool.wait_ge(s_whi, 2 * i + z + 1)
                if wait:
                    pool.wait_ge(s_edn, 10 * i + 5 * z - 5)
                pool.tensor_tensor(ew_lo[z][:], ew[:, z], ew_hi[:, z].bitcast(F32), ALU.subtract).then_inc(s_wlo, 1)

            def expert(i, z, first, more):
                pool.wait_ge(s_xg[z], 16 * i + 16)
                if not first:
                    pool.wait_ge(s_yst[z], 16 * CT * i)
                pool.wait_ge(s_zero, 1)
                pool.tensor_copy(dest[:, z], xg[:, z, :, D]).then_inc(s_dest, 1)
                if more:
                    weights_lo(i + z, 1 - z, not (first and z == 0))
                pool.wait_ge(s_dest, 2 * i + z + 1)
                for t in range(CT):
                    pool.wait_ge(s_eev, 10 * i + 5 * z + t + 1)
                    pool.wait_ge(s_zero, 1)
                    pool.indirect_dma_start(out=results[:, :], out_offset=bass.IndirectOffsetOnAxis(ap=dest[:, z, t:t + 1], axis=0),
                                            in_=yo[:, z, t], in_offset=None, bounds_check=K * N - 1, oob_is_err=False).then_inc(s_yst[z], 16)
            pool.wait_ge(s_yz, 16 * NCH)
            weights_lo(0, 0, False)
            pool.wait_ge(s_smm, 3 * B)
            for e in range(NE):
                expert(e // 2, e % 2, e < 2, e + 1 < NE)

        @block.tensor
        def _(pe):
            pe.wait_ge(s_ps0, 1)
            pe.wait_ge(s_zero, 1)
            zero16 = zero[:].bitcast(BF16)

            def keep_up(columns):
                nc.tensor.matmul(ps[:, 6, 0:columns], zero16[:, 0:P], zero16[:, 0:columns], start=True, stop=True)

            def kernel_sums(piece):
                half, h = piece // NH, piece % NH
                at = slice(half * P // 2, (half + 1) * P // 2)
                for j in range(CG):
                    last = nc.tensor.matmul(ps[Q * j:Q * j + J, 4, at], cblk[:, j, h], qx[:, 0, NH * j + h, at], start=piece == 0, stop=h == NH - 1,
                                            skip_group_check=True, tile_position=(0, Q * j))
                if piece == 2 * NH - 1:
                    last.then_inc(s_kmm, 1)

            def xpart(bank, t):
                for k in range(C):
                    for j in range(J):
                        nc.tensor.matmul(sums_at(bank, t)[Q * j:Q * j + B], xst[:, bank, k, t], wx[:, k, j * W:(j + 1) * W],
                                         start=t < 2 and k == 0, stop=False, skip_group_check=True, tile_position=(0, Q * j))
                for j in range(J):
                    last = nc.tensor.matmul(sums_at(bank, t)[Q * j:Q * j + B], tri[0:1, 1, 0:B], brow[:, j * W:(j + 1) * W],
                                            start=False, stop=False, skip_group_check=True, tile_position=(0, Q * j))
                return last
            for _ in range(WARM):
                keep_up(512)
            pe.wait_ge(s_first, FIRST_LOADED)
            pe.wait_ge(s_xs[0], 16)
            for t in range(G):
                last = xpart(0, t)
            last.then_inc(s_xdone, 1)

            def steps(i, bank, more, kernel):
                for t in range(G):
                    n = bank * G + t
                    for k in range(C):
                        pe.wait_ge(s_h, 4 * G * i + 2 * n + k + 1)
                        for j in range(J):
                            last = nc.tensor.matmul(sums_at(bank, t)[Q * j:Q * j + B], hring[:, (n - 1) % (2 * G), k], wh[:, k, j * W:(j + 1) * W],
                                                    start=False, stop=True, skip_group_check=True, tile_position=(0, Q * j))
                    last.then_inc(s_sum, 1)
                    if more:
                        if t == 0:
                            pe.wait_ge(s_xs[1 - bank], 16 * i + 16 + 16 * bank)
                        last = xpart(1 - bank, t)
                        if t == G - 1:
                            last.then_inc(s_xdone, 1)
                    if kernel and 11 <= n < 11 + 2 * NH:
                        if n == 11:
                            pe.wait_ge(s_ps0, 1)
                            pe.wait_ge(s_kqe, i + 1)
                            pe.wait_ge(s_kc, i + 1)
                        kernel_sums(n - 11)
                        continue
                    keep_up(FILL if more else 512)
            IT = S // G // 2
            with pe.Fori(0, NCH) as i:
                for bank in range(2):
                    steps(i, bank, True, True)
            with pe.Fori(NCH, IT - 1) as i:
                for bank in range(2):
                    steps(i, bank, True, False)
            for bank in range(2):
                steps(IT - 1, bank, bank == 0, False)

            pe.wait_ge(s_hist, 2 * IT + 2)
            pe.wait_ge(s_late, LATE)
            n = 0
            for tb in range(TB):
                for k in range(C):
                    for bq in range(2):
                        if n >= 4:
                            pe.wait_ge((s_uev, s_uea)[n % 2], (n - 4) // 2 + 1)
                        for b in range(4):
                            last = nc.tensor.transpose(ps[:, 2 + n % 4, b * P:(b + 1) * P], uT[:, k, S - (tb + 1) * P:S - tb * P, 4 * bq + b], ident[:])
                        last.then_inc(s_utr, 1)
                        n += 1

            def own_block(s, z, wait):
                pe.wait_ge(s_ust, s + 1)
                pe.wait_ge(s_pe, s + 1)
                pe.wait_ge(s_t0[z], 8 * CG * (s - z) + 16 * CG)
                for g in range(CG):
                    if wait and g % 2 == 0:
                        pe.wait_ge(s_y, 2 * s - 3 + g // 2)
                    o = (g % 2) * (P + NST)
                    for j in range(J):
                        last = nc.tensor.matmul(ps[Q * j:Q * j + Q, 2 * z + g // 2, o:o + P + NST], ust[:, z, g, j], tp[:, z, g, j],
                                                start=g % 2 == 0, stop=False, skip_group_check=True, tile_position=(0, Q * j))
                    if g < CG - 1:
                        keep_up(128)
                last.then_inc(s_tmm, 1)
                keep_up(128)

            def carried(s, z):
                pe.wait_ge(s_ps0, 1)
                pe.wait_ge(s_xc, s + 1)
                pe.wait_ge(s_qe, s + 1)
                for g in range(CG):
                    o = (g % 2) * (P + NST)
                    for h in range(NH):
                        for j in range(J):
                            last = nc.tensor.matmul(ps[Q * j:Q * j + Q, 2 * z + g // 2, o:o + P], xc[Q * j:Q * j + Q, z, NH * g + h], qx[Q * j:Q * j + Q, z, NH * g + h],
                                                    start=False, stop=True, skip_group_check=True, tile_position=(Q * j, Q * j))
                    if g % 2 == 1:
                        last.then_inc(s_qmm, 1)
                    keep_up(128)

            def by_time(s, z, wait):
                pe.wait_ge(s_y, 2 * s + 2)
                if wait:
                    pe.wait_ge(s_x1, s - 1)
                for g in range(CG):
                    last = nc.tensor.transpose(ps[:, 4 + z, g * P:(g + 1) * P], ysb[:, z, g], ident[:])
                last.then_inc(s_ytr, 1)
                keep_up(512)
            pe.wait_ge(s_uev, 8)
            pe.wait_ge(s_uea, 8)
            own_block(0, 0, False)
            own_block(1, 1, False)
            carried(0, 0)
            for s in (2, 3):
                own_block(s, s % 2, True)
                carried(s - 1, 1 - s % 2)
                by_time(s - 2, s % 2, False)
            with pe.Fori(2, NCH // 2) as i:
                for z in range(2):
                    own_block(2 * i + z, z, True)
                    carried(2 * i + z - 1, 1 - z)
                    by_time(2 * i + z - 2, z, True)
            carried(NCH - 1, 1)
            by_time(NCH - 2, 0, True)
            by_time(NCH - 1, 1, True)
            def x1_turned(b):
                for c in range(C):
                    if b >= 4:
                        pe.wait_ge(s_hev, 2 * (b - 4) + c + 1)
                    elif b >= 1:
                        pe.wait_ge(s_x1ev, 2 * (b - 1) + c + 1)
                    for tb in range(TB):
                        last = nc.tensor.transpose(ps[:, 6 + c, tb * P:(tb + 1) * P], xtok[:, 4 * b + tb, c * P:(c + 1) * P], ident[:])
                    last.then_inc(s_x1tr, 1)

            def hid_turned(b):
                pe.wait_ge(s_hid, 2 * b + 2)
                for c in range(C):
                    if b + 3 < B:
                        pe.wait_ge(s_x1ev, 2 * (b + 3) + c + 1)
                    else:
                        pe.wait_ge(s_hev, 2 * (b - 1) + c + 1)
                    for tb in range(TB):
                        last = nc.tensor.transpose(ps[:, 6 + c, tb * P:(tb + 1) * P], hidT[:, c, 4 * b + tb, :], ident[:])
                    last.then_inc(s_htr, 1)
            pe.wait_ge(s_x1, NCH)
            x1_turned(0)
            for b in range(B):
                if 1 <= b < B - 1:
                    x1_turned(b + 1)
                pe.wait_ge(s_x1ev, 2 * b + 2)
                for z in range(2):
                    if b == 0 and z == 1:
                        x1_turned(1)
                    if b >= 1:
                        pe.wait_ge(s_fic, 3 * (2 * b + z) - 3)
                    for q in range(3):
                        for c in range(C):
                            last = nc.tensor.matmul(ps[:, 3 * z + q, :], gw[:, q, c, z * P:(z + 1) * P], x1T[:, c, 4 * b:4 * b + 4, :].rearrange("p r t -> p (r t)"), start=c == 0, stop=c == C - 1)
                    last.then_inc(s_gmm, 1)
                if 2 <= b < B - 1:
                    hid_turned(b - 2)
            pe.wait_ge(s_sw, 48)

            def shared_gate_up(b, f):
                f0, fw = FT[f]
                if b >= EARLY and f == 0:
                    pe.wait_ge(s_swlo, 1)
                    pe.wait_ge(s_shlo, b - EARLY + 1)
                for of, bank in zip((gate_of, up_of), shared_banks(3 * b + f)):
                    for c in range(C):
                        parts = ((sw_hi, sh_hi), (sw_hi, sh_lo), (sw_lo, sh_hi)) if b >= EARLY else ((sw, None),)
                        for p, (w, h) in enumerate(parts):
                            v = h[b % 2][:, c] if h else hidT[:, c, 4 * b:4 * b + 4, :].rearrange("p r t -> p (r t)")
                            last = nc.tensor.matmul(ps[0:fw, bank, :], of(w)[:, c, f0:f0 + fw], v, start=c == 0 and p == 0, stop=c == C - 1 and p == len(parts) - 1)
                last.then_inc(s_smm, 1)

            def shared_down(b):
                if b >= EARLY:
                    pe.wait_ge(s_salo, 3 * (b - EARLY) + 3)
                else:
                    pe.wait_ge(s_sact, 3 * b + 3)
                if b >= 1:
                    pe.wait_ge(s_sacc, b)
                parts = ((sact_hi, sw_hi), (sact_hi, sw_lo), (sact_lo, sw_hi)) if b >= EARLY else ((sact3, sw),)
                for tb in range(TB):
                    for f, (f0, fw) in enumerate(FT):
                        for p, (a, w) in enumerate(parts):
                            last = nc.tensor.matmul(ps[:, 4 + tb // 2, (tb % 2) * D:(tb % 2 + 1) * D], a[0:fw, f, tb * P:(tb + 1) * P], down_of(w)[0:fw, f],
                                                    start=f == 0 and p == 0, stop=f == 2 and p == len(parts) - 1)
                last.then_inc(s_sdn, 1)
            pe.wait_ge(s_fic, 6 * B - 3)
            shared_gate_up(0, 0)
            hid_turned(B - 3)
            pe.wait_ge(s_fic, 6 * B)
            shared_gate_up(0, 1)

            def logits(b):
                for c in range(C):
                    last = nc.tensor.matmul(ps[Q * (b % J):Q * (b % J) + NE, 4 + b // J, :].rearrange("p (r t) -> p r t", r=TB), rw[:, c], hidT[:, c, 4 * b:4 * b + 4, :],
                                            start=c == 0, stop=c == C - 1, tile_position=(0, Q * (b % J)))
                return last
            for b in range(B - 2):
                logits(b)
            hid_turned(B - 2)
            pe.wait_ge(s_hid, 2 * B)
            for b in range(B - 2, B):
                last = logits(b)
            last.then_inc(s_lg, 1)
            pe.wait_ge(s_lge, 1)
            pe.wait_ge(s_ssil, 1)
            for q in range(2):
                for tb in range(TB):
                    last = nc.tensor.transpose(ps[:, 2 * q, tb * P:(tb + 1) * P], lgT[:, q, tb * P:(tb + 1) * P], ident[:])
            last.then_inc(s_ltr, 1)
            hid_turned(B - 1)
            pe.wait_ge(s_ssil, 2)
            shared_gate_up(0, 2)

            def inputs_turned(i, z, units):
                pe.wait_ge(s_xg[z], 16 * i + 16)
                for u in units:
                    if u == 2:
                        pe.wait_ge(s_xev, 6 * i + 3 * z + 1)
                    for c, t, bank, at in TURNS[u]:
                        last = nc.tensor.transpose(ps[:, bank, at * P:(at + 1) * P], xg[:, z, t, c * P:(c + 1) * P], ident[:])
                    last.then_inc(s_xtr, 1)

            def shared_next(b, f):
                nf = 3 * b + f
                if nf == 3:
                    pe.wait_ge(s_z, 1)
                elif nf - 2 < 3 * EARLY:
                    pe.wait_ge(s_ssil, nf - 1)
                else:
                    pe.wait_ge(s_sact, nf - 1)
                shared_gate_up(b, f)
            for b in range(B):
                if b >= 1:
                    shared_next(b, 1)
                    shared_next(b, 2)
                if b == 1:
                    pe.wait_ge(s_cnt, 1)
                    pe.wait_ge(s_hev, 2 * B)
                    for h in range(2):
                        last = nc.tensor.matmul(ps[:, 6 + h, :], tri[:, h], rt[:, 9], start=True, stop=True)
                    last.then_inc(s_rank, 1)
                if b + 1 < B:
                    shared_next(b + 1, 0)
                if b == B - 1:
                    inputs_turned(0, 0, (0, 1))
                shared_down(b)

            def expert(i, z, first, more):
                pe.wait_ge(s_xev, 6 * i + 3 * z + 3)
                pe.wait_ge(s_wlo, 2 * i + z + 1)
                for m in range(6):
                    hf, f = m // 3, m % 3
                    f0, fw = FT[f]
                    if not (first and m < 2):
                        pe.wait_ge(s_eact, 12 * i + 6 * z + m - 1)
                    for h, of in enumerate((gate_of, up_of)):
                        for c in range(C):
                            for p, (w, v) in enumerate(((ew_hi[:, z], xgT_hi), (ew_hi[:, z], xgT_lo), (ew_lo[z], xgT_hi))):
                                last = nc.tensor.matmul(ps[0:fw, 2 * h + m % 2, 0:HALF], of(w)[:, c, f0:f0 + fw], v[:, c, hf * HALF:(hf + 1) * HALF],
                                                        start=c == 0 and p == 0, stop=c == C - 1 and p == 2)
                    last.then_inc(s_emm, 1)
                if more:
                    inputs_turned(i + z, 1 - z, (0, 1))
                for t in range(CT):
                    pe.wait_ge(s_elo, 12 * i + 6 * z + (3 if (t + 1) * P <= HALF else 6))
                    if not (first and t < 2):
                        pe.wait_ge(s_eev, 10 * i + 5 * z + t - 1)
                    for f, (f0, fw) in enumerate(FT):
                        for p, (a, w) in enumerate(((eact_hi, ew_hi[:, z]), (eact_hi, ew_lo[z]), (eact_lo, ew_hi[:, z]))):
                            last = nc.tensor.matmul(ps[:, 4 + (z + t) % 2, 0:D], a[0:fw, f, t * P:(t + 1) * P], down_of(w)[0:fw, f], start=f == 0 and p == 0, stop=f == 2 and p == 2)
                    last.then_inc(s_edn, 1)
                    if more and t == 2:
                        inputs_turned(i + z, 1 - z, (2,))
            inputs_turned(0, 0, (2,))
            for z in range(2):
                expert(0, z, z == 0, True)
            with pe.Fori(1, NE // 2 - 1) as i:
                for z in range(2):
                    expert(i, z, False, True)
            for z in range(2):
                expert(NE // 2 - 1, z, False, z == 0)

        @block.scalar
        def _(act):
            act.preload_act_table(ACT.Tanh)
            act.wait_ge(s_const, LOADED)
            nc.scalar.activation(a_bc[:], a_bc[:], ACT.Exp).then_inc(s_dtm, 1)
            nc.scalar.activation(a_q[:], a_q[:], ACT.Exp).then_inc(s_dtm, 1)
            nc.scalar.activation(dt_bc[:], dt_bc[:], ACT.Exp).then_inc(s_dtm, 1)
            nc.scalar.activation(dt_q[:], dt_q[:], ACT.Exp).then_inc(s_dtm, 1)
            act.wait_ge(s_dta, 1)
            nc.scalar.activation(lam[:], dta_q[:], ACT.Exp, scale=-float(P)).then_inc(s_lam, 1)
            def steps(i, kernel, conv=False):
                for n in range(2 * G):
                    if n % G == 0:
                        act.wait_ge(s_hist, 2 * i + n // G + 1)
                    for k in range(C):
                        act.wait_ge(s_zt, 4 * G * i + 2 * n + k + 1)
                        nc.scalar.activation(hring[:, n, k], zt[:, n % 2, k * Q:k * Q + B], ACT.Tanh).then_inc(s_h, 1)
                    if kernel and 2 <= n < 2 + CG * NH:
                        if n == 2:
                            act.wait_ge(s_kq, i + 1)
                        last = nc.scalar.activation(qx[:, 0, n - 2], qx[:, 0, n - 2], ACT.Exp, scale=-1.0)
                        if n == 1 + CG * NH:
                            last.then_inc(s_kqe, 1)
                    if conv:
                        first_args(n)
            with act.Fori(0, NCH) as i:
                steps(i, True)

            def first_args(n):
                z, decay, g = n // (2 * CG), n // CG % 2, n % CG
                if n == 0:
                    act.wait_ge(s_pa, 2)
                    act.wait_ge(s_qa, 2)
                if decay:
                    last = nc.scalar.activation(qx[:, z, NH * g:NH * g + NH], qx[:, z, NH * g:NH * g + NH], ACT.Exp, scale=-1.0)
                else:
                    last = nc.scalar.activation(tp[:, z, g, :, P:P + NST], tp[:, z, g, :, P:P + NST], ACT.Exp, scale=consts[:, 4:5])
                if g == CG - 1:
                    last.then_inc(s_qe if decay else s_pe, 1)
            with act.Fori(NCH, S // G // 2 - 1) as i:
                steps(i, False)
            steps(S // G // 2 - 1, False, True)

            u_out(act, lambda to, v: nc.scalar.activation(to, v, ACT.Copy), 1, s_uea)

            def powers(s, z):
                act.wait_ge(s_pa, s + 1)
                nc.scalar.activation(tp[:, z, :, :, P:P + NST], tp[:, z, :, :, P:P + NST], ACT.Exp, scale=consts[:, 4:5]).then_inc(s_pe, 1)

            def decays(s, z):
                act.wait_ge(s_qa, s + 1)
                nc.scalar.activation(qx[:, z], qx[:, z], ACT.Exp, scale=-1.0).then_inc(s_qe, 1)

            def sums_out(s, z, hb, wait):
                if wait and hb == 0:
                    act.wait_ge(s_ytr, s - 1)
                act.wait_ge(s_qmm, 2 * s + hb + 1)
                nc.scalar.activation(ysb[:, z, 2 * hb:2 * hb + 2], ps[:, 2 * z + hb, 0:2 * (P + NST)].rearrange("p (g t) -> p g t", g=2)[:, :, 0:P], ACT.Copy).then_inc(s_y, 1)
            for s in range(2):
                sums_out(s, s, 0, False)
                powers(s + 2, s)
                sums_out(s, s, 1, False)
                decays(s + 2, s)
            with act.Fori(1, NCH // 2 - 1) as i:
                for z in range(2):
                    sums_out(2 * i + z, z, 0, True)
                    powers(2 * i + z + 2, z)
                    sums_out(2 * i + z, z, 1, True)
                    decays(2 * i + z + 2, z)
            for z in range(2):
                for hb in range(2):
                    sums_out(NCH - 2 + z, z, hb, True)
            act.preload_act_table(ACT.Sigmoid)

            def x1_out(b):
                for c in range(C):
                    act.wait_ge(s_zero, 1)
                    act.wait_ge(s_x1tr, 2 * b + c + 1)
                    nc.scalar.activation(x1T[:, c, bass.ds(TB * b, TB), :], ps[:, 6 + c, :].rearrange("p (r t) -> p r t", r=TB), ACT.Copy).then_inc(s_x1ev, 1)

            def gates(n, z, wait):
                act.wait_ge(s_gmm, n + 1)
                if wait:
                    act.wait_ge(s_new, n - 1)
                for q, function in enumerate((ACT.Sigmoid, ACT.Sigmoid, ACT.Identity)):
                    nc.scalar.activation(gbuf[:, z, q if q < 2 else 3], ps[:, 3 * z + q, :], function, bias=gb[:, q, z:z + 1]).then_inc(s_fic, 1)

            def hid_out(b):
                for c in range(C):
                    act.wait_ge(s_zero, 1)
                    act.wait_ge(s_htr, 2 * b + c + 1)
                    nc.scalar.activation(hid_tok[:, bass.ds(TB * b, TB), c * P:(c + 1) * P], ps[:, 6 + c, :].rearrange("p (r d) -> p r d", r=TB), ACT.Copy).then_inc(s_hev, 1)
            act.wait_ge(s_zf, 16 * NE)
            x1_out(0)
            gates(0, 0, False)
            x1_out(1)
            gates(1, 1, False)
            x1_out(2)
            for z in range(2):
                gates(2 + z, z, True)
            with act.Fori(2, B - 1) as b:
                x1_out(b + 1)
                for z in range(2):
                    gates(2 * b + z, z, True)
                hid_out(b - 2)
            act.wait_ge(s_sw, 48)
            nc.scalar.activation(sw_hi[:], sw, ACT.Copy).then_inc(s_swhi, 1)
            for z in range(2):
                gates(2 * B - 2 + z, z, True)
            hid_out(B - 3)
            def shared_silu(nf):
                fw = FT[nf % 3][1]
                act.wait_ge(s_smm, nf + 1)
                gate, up = shared_banks(nf)
                if nf >= 3 * EARLY:
                    if nf >= 3 * EARLY + 2:
                        act.wait_ge(s_salo, nf - 3 * EARLY - 1)
                    nc.scalar.activation(ssil[0:fw, nf % 2], ps[0:fw, gate, :], ACT.Silu).then_inc(s_ssil, 1)
                    return
                if nf >= 3:
                    act.wait_ge(s_sact, nf - 2)
                nc.scalar.activation(early_sil[0:fw, nf % 3], ps[0:fw, gate, :], ACT.Silu)
                nc.scalar.activation(early_up[0:fw, nf % 3], ps[0:fw, up, :], ACT.Copy).then_inc(s_ssil, 1)
            for nf in range(2):
                shared_silu(nf)
            hid_out(B - 2)
            act.wait_ge(s_lg, 1)
            act.wait_ge(s_hid, 2 * B)
            nc.scalar.activation(lgT, ps[:, 4:6, :], ACT.Copy).then_inc(s_lge, 1)
            hid_out(B - 1)
            act.wait_ge(s_z, 1)
            nc.scalar.activation(rt[:, 1], rt[:, 1], ACT.Exp).then_inc(s_e, 1)
            act.preload_act_table(ACT.Silu)

            def weights_hi(i, z, parts):
                if 0 in parts:
                    act.wait_ge(s_ew[z], 48 * i + 48)
                for p in parts:
                    at = (gate_of, up_of, down_of)[p]
                    last = nc.scalar.activation(at(ew_hi[:, z]), at(ew[:, z]), ACT.Copy)
                if 2 in parts:
                    last.then_inc(s_whi, 1)

            def inputs_hi(i, z, units):
                for u in units:
                    act.wait_ge(s_xtr, 6 * i + 3 * z + u + 1)
                    c, t, bank, at = TURNS[u][0]
                    n = len(TURNS[u])
                    if u < 2:
                        ins = nc.scalar.activation(xgT_hi[:, u, 0:n * P], ps[:, bank, 0:n * P], ACT.Copy)
                    else:
                        ins = nc.scalar.activation(xgT_hi[:, :, t * P:(t + 1) * P], ps[:, bank, at * P:(at + n) * P].rearrange("p (c t) -> p c t", c=C), ACT.Copy)
                    ins.then_inc(s_xhi, 1)

            def expert(i, z, first, more):
                def product_hi(m):
                    hf, f = m // 3, m % 3
                    fw = FT[f][1]
                    act.wait_ge(s_eact, 12 * i + 6 * z + m + 1)
                    nc.scalar.activation(eact_hi[0:fw, f, hf * HALF:(hf + 1) * HALF], eprod[0:fw, m % 2], ACT.Copy).then_inc(s_ehi, 1)

                def results_out(t):
                    act.wait_ge(s_edn, 10 * i + 5 * z + t + 1)
                    if t == 0 and not isinstance(i, int) or t == 0 and i > 0:
                        act.wait_ge(s_yst[z], 16 * CT * i)
                    nc.scalar.activation(yo[:, z, t], ps[:, 4 + (z + t) % 2, 0:D], ACT.Copy).then_inc(s_eev, 1)
                for m in range(6):
                    fw = FT[m % 3][1]
                    act.wait_ge(s_emm, 12 * i + 6 * z + m + 1)
                    if not (first and m < 2):
                        act.wait_ge(s_eact, 12 * i + 6 * z + m - 1)
                    nc.scalar.activation(esil[0:fw, m % 2], ps[0:fw, m % 2, 0:HALF], ACT.Silu).then_inc(s_esil, 1)
                    if m >= 1:
                        product_hi(m - 1)
                    if more and 1 <= m <= 3:
                        weights_hi(i + z, 1 - z, (m - 1,))
                product_hi(5)
                if more:
                    inputs_hi(i + z, 1 - z, (0, 1))
                for t in range(CT):
                    results_out(t)
                    if more and t == 2:
                        inputs_hi(i + z, 1 - z, (2,))
            def shared_hidden_hi(b):
                if b == EARLY + 1:
                    act.wait_ge(s_sact, 3 * EARLY)
                nc.scalar.activation(sh_hi[b % 2][:], hidT[:, :, 4 * b:4 * b + 4, :].rearrange("p c r t -> p c (r t)"), ACT.Copy).then_inc(s_shhi, 1)

            def shared_product_hi(nf):
                b, f = nf // 3, nf % 3
                fw = FT[f][1]
                act.wait_ge(s_sact, nf + 1)
                if f == 0:
                    act.wait_ge(s_sdn, b)
                nc.scalar.activation(sact_hi[0:fw, f], ssil[0:fw, nf % 2], ACT.Copy).then_inc(s_sahi, 1)
            shared_silu(2)
            for b in range(1, B):
                for f in range(3):
                    nf = 3 * b + f
                    shared_silu(nf)
                    if f == 0 and EARLY <= b + 1 < B:
                        shared_hidden_hi(b + 1)
                    if b >= EARLY and f >= 1:
                        shared_product_hi(nf - 1)
                if b >= EARLY:
                    shared_product_hi(3 * b + 2)
            act.wait_ge(s_sc, 16 * R * K)
            weights_hi(0, 0, (0, 1, 2))
            inputs_hi(0, 0, (0, 1, 2))
            for z in range(2):
                expert(0, z, z == 0, True)
            with act.Fori(1, NE // 2 - 1) as i:
                for z in range(2):
                    expert(i, z, False, True)
            for z in range(2):
                expert(NE // 2 - 1, z, False, z == 0)

        @block.vector
        def _(dve):
            chain = [0]

            def link(ins):
                ins.then_inc(s_c, 1)
                chain[0] = chain[0] + 1
                dve.wait_ge(s_c, chain[0])

            nc.vector.memset(ps[:, 0:5], 0.0).then_inc(s_ps0, 1)
            nc.vector.memset(xc[:], 0.0).then_inc(s_hist, 2)
            dve.wait_ge(s_first, FIRST_LOADED)
            nc.vector.tensor_copy(hring[:, 2 * G - 1], h0r[:]).then_inc(s_h, 2)
            dve.wait_ge(s_const, LOADED)
            dve.wait_ge(s_dtm, 4)
            nc.vector.tensor_tensor(dta_q[:], dt_q[:].unsqueeze(2).to_broadcast([P, NG, NH]), a_q[:].unsqueeze(1).to_broadcast([P, NG, NH]), ALU.mult).then_inc(s_dta, 1)

            def kernel_states(i):
                c = c_q[:, bass.ds(CG * i, CG), :].rearrange("p g h -> p (g h)")
                nc.vector.tensor_tensor(cblk.rearrange("p g h j -> p (g h) j"), c.unsqueeze(2).to_broadcast([P, CG * NH, J]), consts[:, 0:J].unsqueeze(1).to_broadcast([P, CG * NH, J]), ALU.mult).then_inc(s_kc, 1)

            def kernel_out(i):
                dve.wait_ge(s_kmm, i + 1)
                dve.wait_ge(s_kst, 16 * CG * i + 16)
                nc.vector.tensor_scalar(ksb[:, 1:P], ps[:, 4, 1:P], 1.0, None, ALU.mult)
                nc.vector.tensor_tensor(ksb[:, 0:1], ps[:, 4, 0:1], d_k[:, bass.ds(i, 1)], ALU.add).then_inc(s_kev, 1)

            IT = S // G // 2

            def turn(i, n):
                dve.wait_ge(s_sum, 2 * G * i + n + 1)
                bank, t = n // G, n % G
                for k in range(C):
                    nc.vector.transpose(zt[:, n % 2, k * Q:(k + 1) * Q], sums_at(bank, t)[:, k * Q:(k + 1) * Q]).then_inc(s_zt, 1)
            def steps(i, kernel):
                for n in range(2 * G):
                    turn(i, n)
                    if kernel and n == 4:
                        kernel_states(i)
                    if kernel and n == 15:
                        kernel_out(i)
            with dve.Fori(0, NCH) as i:
                steps(i, True)
            with dve.Fori(NCH, IT) as i:
                steps(i, False)
            u_out(dve, lambda to, v: nc.vector.tensor_copy(to, v), 0, s_uev)

            def states(z, chunk):
                nc.vector.tensor_scalar(ust[:, z].rearrange("p g j r -> p (g j r)"), u_tok[:, bass.ds(CG * chunk, CG)].rearrange("p g j r -> p (g j r)"), 1.0, None, ALU.mult).then_inc(s_ust, 1)

            def carry(chunk, z):
                dve.wait_ge(s_tmm, chunk + 1)
                for hb in range(2):
                    last = nc.vector.transpose(stt[:, z].rearrange("p (hb gn) r -> p hb (gn r)", hb=2)[:, hb].rearrange("p (g n) -> p g n", g=2),
                                               ps[:, 2 * z + hb, 0:2 * (P + NST)].rearrange("p (g t) -> p g t", g=2)[:, :, P:P + NST])
                link(last)
                sv = stt[:, z].rearrange("p n (b t) -> p n b t", t=TB)
                lv = lam[:, bass.ds(CG * chunk, CG), :].rearrange("p g h -> p (g h)").unsqueeze(2).to_broadcast([P, CG * NH, B])
                for tb in range(1, TB - 1):
                    link(nc.vector.tensor_tensor(ctmp, sv[:, :, :, tb - 1], lv, ALU.mult))
                    link(nc.vector.tensor_tensor(sv[:, :, :, tb], sv[:, :, :, tb], ctmp, ALU.add))
                cv = c_q[:, bass.ds(CG * chunk, CG), :].rearrange("p g h -> p (g h)").unsqueeze(2).unsqueeze(3).to_broadcast([P, CG * NH, B, TB - 1])
                nc.vector.tensor_tensor(xc[:, z].rearrange("p n (b t) -> p n b t", t=TB)[:, :, :, 1:TB], sv[:, :, :, 0:TB - 1], cv, ALU.mult).then_inc(s_xc, 1)

            def add_x(chunk, z):
                dve.wait_ge(s_ytr, chunk + 1)
                for j in range(J):
                    xv = xtok[:, :, bass.ds(NG * j + CG * chunk, CG)].rearrange("p r g -> p g r")
                    last = nc.vector.tensor_tensor(xv, ps[:, 4 + z, :].rearrange("p (g j r) -> p j g r", g=CG, j=J)[:, j], xv, ALU.add)
                last.then_inc(s_x1, 1)
            dve.wait_ge(s_uev, 8)
            dve.wait_ge(s_uea, 8)
            dve.wait_ge(s_x, 16 * PIECES)
            PER = 5
            base = chain[0]
            for z in range(2):
                states(z, z)
            for s in range(2):
                carry(s, s)
                states(s, s + 2)
            assert chain[0] == base + 2 * PER
            with dve.Fori(1, NCH // 2 - 1) as i:
                chain[0] = i * (2 * PER) + base
                for z in range(2):
                    carry(2 * i + z, z)
                    states(z, 2 * i + z + 2)
                    add_x(2 * i + z - 2, z)
            chain[0] = base + PER * (NCH - 2)
            for z in range(2):
                carry(NCH - 2 + z, z)
                add_x(NCH - 4 + z, z)
            for z in range(2):
                add_x(NCH - 2 + z, z)
            zeros = zero[:]

            def sums(n, z):
                dve.wait_ge(s_w, n + 1)
                nc.vector.tensor_tensor_scan(gbuf[:, z, 7], gbuf[:, z, 5], zeros, 0.0, ALU.add, ALU.add).then_inc(s_cs, 1)

            def divide(n, z):
                v = lambda m: gbuf[:, z, m]
                dve.wait_ge(s_fic, 3 * n + 2)
                link(nc.vector.scalar_tensor_tensor(v(2), v(0), EPS, v(1), ALU.add, ALU.add))
                nc.vector.reciprocal(v(2), v(2)).then_inc(s_r, 1)

            def products(n, b, z):
                v = lambda m: gbuf[:, z, m]
                dve.wait_ge(s_ap, n + 1)
                link(nc.vector.tensor_scalar(v(4), v(4), EPS, None, ALU.add))
                nc.vector.tensor_tensor_scan(v(7)[:, ::-1], v(4)[:, ::-1], zeros, 1.0, ALU.mult, ALU.add).then_inc(s_q, 1)
                nc.vector.tensor_tensor_scan(v(6), v(4), zeros, h0g[:, z, bass.ds(b, 1)], ALU.mult, ALU.add)
            base = chain[0]
            divide(0, 0)
            divide(1, 1)
            products(0, 0, 0)
            assert chain[0] == base + 3
            with dve.Fori(1, B) as b:
                chain[0] = b * 4 + (base - 1)
                for z in range(2):
                    divide(2 * b + z, z)
                    sums(2 * b + z - 2, z)
                    products(2 * b + z - 1, b - (1 - z), 1 - z)
            chain[0] = base + 4 * B - 1
            sums(2 * B - 2, 0)
            products(2 * B - 1, B - 1, 1)
            sums(2 * B - 1, 1)
            def shared_sum(b):
                dve.wait_ge(s_sdn, b + 1)
                if b < HADD:
                    dve.wait_ge(s_hadd, 2 * b + 2)
                else:
                    dve.wait_ge(s_hadd2, b - HADD + 1)
                for q in range(2):
                    last = nc.vector.tensor_tensor(xtok[:, 4 * b + 2 * q:4 * b + 2 * q + 2, :], ps[:, 4 + q, :].rearrange("p (r d) -> p r d", r=2), xtok[:, 4 * b + 2 * q:4 * b + 2 * q + 2, :], ALU.add)
                last.then_inc(s_sacc, 1)

            def shared_hidden_lo(b):
                dve.wait_ge(s_shhi, b - EARLY + 1)
                nc.vector.tensor_tensor(sh_lo[b % 2][:], hidT[:, :, 4 * b:4 * b + 4, :].rearrange("p c r t -> p c (r t)"), sh_hi[b % 2][:].bitcast(F32), ALU.subtract).then_inc(s_shlo, 1)

            v = lambda m: rt[:, m].rearrange("p (r e) -> p r e", e=NE)
            row = lambda m: sm[:, m]
            wide = lambda m: sm[:, m].unsqueeze(2).to_broadcast([P, R, NE])
            each = lambda a: a.unsqueeze(1).to_broadcast([P, R, NE])
            dve.wait_ge(s_ltr, 1)
            for q in range(2):
                for tb in range(TB):
                    last = nc.vector.tensor_tensor(v(0).rearrange("p (b t) e -> p b t e", t=TB)[:, J * q:J * q + J, tb], ps[:, 2 * q, tb * P:(tb + 1) * P].rearrange("p (j e) -> p j e", j=J)[:, :, 0:NE],
                                                   rb[:].unsqueeze(1).to_broadcast([P, J, NE]), ALU.add)
            link(last)
            link(nc.vector.tensor_reduce(row(0), v(0), AX.X, ALU.max))
            nc.vector.tensor_tensor(v(1), v(0), wide(0), ALU.subtract).then_inc(s_z, 1)
            dve.wait_ge(s_e, 1)
            link(nc.vector.tensor_reduce(row(1), v(1), AX.X, ALU.add))
            link(nc.vector.reciprocal(row(2), row(1)))
            link(nc.vector.tensor_tensor(v(2), v(1), wide(2), ALU.mult))
            for k in range(K):
                p, val, at, eq, oh = 2 + 4 * k, 3 + k, 5 + k, 3, 4 + k
                if k == 1:
                    link(nc.vector.scalar_tensor_tensor(v(p), v(4), -4.0, v(2), ALU.mult, ALU.add))
                link(nc.vector.tensor_reduce(row(val), v(p), AX.X, ALU.max))
                link(nc.vector.tensor_tensor(v(eq), v(p), wide(val), ALU.is_equal))
                link(nc.vector.scalar_tensor_tensor(v(eq), v(eq), -float(NE), each(iota_e[:, 0]), ALU.mult, ALU.add))
                link(nc.vector.tensor_reduce(row(at), v(eq), AX.X, ALU.min))
                link(nc.vector.tensor_tensor(v(oh), each(iota_e[:, 1]), wide(at), ALU.is_equal))
            nc.vector.tensor_tensor(v(9), v(4), v(5), ALU.add).then_inc(s_cnt, 1)
            link(nc.vector.tensor_tensor(row(11), row(3), row(4), ALU.add))
            link(nc.vector.tensor_scalar(row(11), row(11), 1e-9, None, ALU.add))
            link(nc.vector.reciprocal(row(11), row(11)))
            both = lambda m: sm[:, m:m + K]
            link(nc.vector.tensor_tensor(both(12), both(3), row(11).unsqueeze(1).to_broadcast([P, K, R]), ALU.mult))
            shared_sum(0)
            shared_hidden_lo(EARLY)
            dve.wait_ge(s_rank, 1)
            by_e = lambda m: rt[:, m].rearrange("p (e r) -> p e r", r=R)
            link(nc.vector.tensor_copy(by_e(7), ps[:, 7, :].rearrange("p (r e) -> p e r", e=NE)))
            link(nc.vector.tensor_tensor_scan(rt[:, 8], resets[:].rearrange("p e r -> p (e r)"), rt[:, 7], 0.0, ALU.mult, ALU.add))
            link(nc.vector.tensor_tensor(v(3), ps[:, 6, :].rearrange("p (r e) -> p r e", e=NE), by_e(8).rearrange("p e r -> p r e"), ALU.add))
            link(nc.vector.tensor_tensor(rt[:, 10:10 + K], rt[:, 4:4 + K], rt[:, 3].unsqueeze(1).to_broadcast([P, K, R * NE]), ALU.mult))
            link(nc.vector.tensor_reduce(both(7), rt[:, 10:10 + K].rearrange("p k (r e) -> p k r e", e=NE), AX.X, ALU.add))
            nc.vector.tensor_scalar(both(9), both(7), float(CAP), None, ALU.is_lt)
            link(nc.vector.tensor_scalar(both(14), both(7), float(CAP - 1), float(NE * CAP), ALU.min, ALU.add))
            nc.vector.scalar_tensor_tensor(both(14), both(5), float(CAP), both(14), ALU.mult, ALU.add)
            link(nc.vector.tensor_scalar(both(7), both(9), -float(2 * NE * CAP), float(2 * NE * CAP), ALU.mult, ALU.add))
            nc.vector.tensor_tensor(idx[:, 0:K], both(7), both(14), ALU.add).then_inc(s_idx, 1)
            nc.vector.tensor_tensor(wt[:, 0:K], both(12), both(9), ALU.mult).then_inc(s_wt, 1)

            def shared_product_lo(nf):
                f, fw = nf % 3, FT[nf % 3][1]
                dve.wait_ge(s_sahi, nf - 3 * EARLY + 1)
                nc.vector.tensor_tensor(sact_lo[0:fw, f], ssil[0:fw, nf % 2], sact_hi[0:fw, f].bitcast(F32), ALU.subtract).then_inc(s_salo, 1)
            for b in range(1, B):
                if b >= EARLY:
                    for f, (f0, fw) in enumerate(FT):
                        nf = 3 * b + f
                        dve.wait_ge(s_ssil, nf + 1)
                        nc.vector.tensor_tensor(ssil[0:fw, nf % 2], ssil[0:fw, nf % 2], ps[0:fw, shared_banks(nf)[1], :], ALU.mult).then_inc(s_sact, 1)
                        if f == 0 and b + 1 < B:
                            shared_hidden_lo(b + 1)
                        if f >= 1:
                            shared_product_lo(nf - 1)
                    shared_product_lo(3 * b + 2)
                if b < B - 1:
                    shared_sum(b)
                if b >= 1 and HADD <= b + 2 < B:
                    rows = slice(TB * (b + 2), TB * (b + 3))
                    nc.vector.tensor_tensor(xtok[:, rows], xtok[:, rows], hid_tok[:, rows, 0:D], ALU.add).then_inc(s_hadd2, 1)

            def inputs_lo(i, z):
                for u, tiles in enumerate(TURNS):
                    dve.wait_ge(s_xhi, 6 * i + 3 * z + u + 1)
                    c, t, bank, at = tiles[0]
                    n = len(tiles)
                    if u < 2:
                        ins = nc.vector.tensor_tensor(xgT_lo[:, u, 0:n * P], ps[:, bank, 0:n * P], xgT_hi[:, u, 0:n * P].bitcast(F32), ALU.subtract)
                    else:
                        ins = nc.vector.tensor_tensor(xgT_lo[:, :, t * P:(t + 1) * P], ps[:, bank, at * P:(at + n) * P].rearrange("p (c t) -> p c t", c=C),
                                                      xgT_hi[:, :, t * P:(t + 1) * P].bitcast(F32), ALU.subtract)
                    ins.then_inc(s_xev, 1)

            def expert(i, z, first, more):
                def product_lo(m):
                    hf, f = m // 3, m % 3
                    fw = FT[f][1]
                    dve.wait_ge(s_ehi, 12 * i + 6 * z + m + 1)
                    at = slice(hf * HALF, (hf + 1) * HALF)
                    nc.vector.tensor_tensor(eact_lo[0:fw, f, at], eprod[0:fw, m % 2], eact_hi[0:fw, f, at].bitcast(F32), ALU.subtract).then_inc(s_elo, 1)
                for m in range(6):
                    fw = FT[m % 3][1]
                    dve.wait_ge(s_esil, 12 * i + 6 * z + m + 1)
                    if not (first and m < 2):
                        dve.wait_ge(s_elo, 12 * i + 6 * z + m - 1)
                    nc.vector.tensor_tensor(eprod[0:fw, m % 2], esil[0:fw, m % 2], ps[0:fw, 2 + m % 2, 0:HALF], ALU.mult).then_inc(s_eact, 1)
                    if m >= 1:
                        product_lo(m - 1)
                product_lo(5)
                if more:
                    inputs_lo(i + z, 1 - z)
            inputs_lo(0, 0)
            shared_sum(B - 1)
            for z in range(2):
                expert(0, z, z == 0, True)
            with dve.Fori(1, NE // 2 - 1) as i:
                for z in range(2):
                    expert(i, z, False, True)
            for z in range(2):
                expert(NE // 2 - 1, z, False, z == 0)
            dve.wait_ge(s_wt, 1)
            for g in range(R // BACK):
                dve.wait_ge(s_back[g], 16 * K)
                for k in range(K):
                    for r in range(BACK * g, BACK * g + BACK):
                        if k >= 1:
                            dve.wait_ge(s_comb, K * BACK * g + (k - 1) * BACK + r % BACK + 1)
                        nc.vector.scalar_tensor_tensor(xtok[:, r], back[k][:, r], wt[:, k, r:r + 1], xtok[:, r], ALU.mult, ALU.add).then_inc(s_comb, 1)





def kernel(x, cond_1024, L0_cond_Wx, L0_cond_Wh, L0_cond_b, L0_attn_A_log, L0_attn_D, L0_attn_C_re, L0_attn_C_im,
           L0_attn_log_dt, L0_cond2_W_f, L0_cond2_b_f, L0_cond2_W_i, L0_cond2_b_i, L0_cond2_W_h, L0_cond2_b_h,
           L0_ffn_router_w, L0_ffn_router_b, L0_ffn_w_gate, L0_ffn_w_up, L0_ffn_w_down, L0_ffn_sw_gate,
           L0_ffn_sw_up, L0_ffn_sw_down):
    import numpy as np
    import concourse.bacc as bacc
    from concourse.bass_utils import run_bass_kernel_spmd

    f32 = np.float32

    def rows(w):
        return np.asarray(w).reshape(C, P, -1).transpose(1, 0, 2)

    def rec(w):
        return np.asarray(w).reshape(J, C, Q, -1).transpose(0, 2, 1, 3).reshape(P, C, -1)

    def down(w):
        w = np.asarray(w)
        w = np.concatenate([w, np.zeros((3 * P - F, D), f32)])
        return w.reshape(3, P, D).transpose(1, 0, 2)

    x = np.asarray(x)
    cond = np.asarray(cond_1024)
    a_log, c_re, dt = np.asarray(L0_attn_A_log), np.asarray(L0_attn_C_re), np.asarray(L0_attn_log_dt)
    d_k = np.zeros((J, Q, NCH), f32)
    d_k[:, :J] = np.asarray(L0_attn_D).reshape(J, NCH, CG).transpose(2, 0, 1)
    consts = np.zeros((P, 8), f32)
    consts[np.arange(P), np.arange(P) // Q] = 1
    consts[:, 4] = -(np.arange(P) + 1)
    resets = np.ones((P, NE, R), f32)
    resets[:, :, 0] = 0
    iota_e = np.stack([np.arange(NE), np.arange(NE) - NE]).astype(f32)
    tri = np.stack([np.triu(np.ones((P, P)), 1) - 1, np.ones((P, P))], 1).astype(f32)
    arrays = {
        "x_tok": x.reshape(B, TB, P, D).transpose(2, 0, 1, 3).reshape(P, R, D),
        "x_steps": x.reshape(B, S // G, G, C, P).transpose(1, 4, 3, 2, 0),
        "h0_rec": rec(cond.T),
        "h0_gate": rows(cond.T),
        "wx": rows(L0_cond_Wx),
        "wh": rec(L0_cond_Wh),
        "b_rec": np.asarray(L0_cond_b)[None],
        "a_bc": np.broadcast_to(a_log, (P, NST)),
        "a_q": np.tile(a_log.reshape(NH, Q).T, (J, 1)),
        "dt_bc": np.broadcast_to(dt.reshape(J, NG).T, (P, NG, J)),
        "dt_q": np.repeat(dt.reshape(J, NG), Q, 0),
        "c_q": c_re.reshape(J, NG, NH, Q).transpose(0, 3, 1, 2).reshape(P, NG, NH),
        "d_k": d_k.reshape(P, NCH),
        "gate_w": np.stack([rows(np.asarray(w).T) for w in (L0_cond2_W_f, L0_cond2_W_i, L0_cond2_W_h)], 1),
        "gate_b": np.stack([np.asarray(v).reshape(C, P).T for v in (L0_cond2_b_f, L0_cond2_b_i, L0_cond2_b_h)], 1),
        "router_w": rows(L0_ffn_router_w),
        "router_b": np.broadcast_to(np.asarray(L0_ffn_router_b), (P, NE)),
        "sh_gate": rows(L0_ffn_sw_gate),
        "sh_up": rows(L0_ffn_sw_up),
        "sh_down": down(L0_ffn_sw_down),
        "ex_gate": np.stack([rows(w) for w in np.asarray(L0_ffn_w_gate)]),
        "ex_up": np.stack([rows(w) for w in np.asarray(L0_ffn_w_up)]),
        "ex_down": np.stack([down(w) for w in np.asarray(L0_ffn_w_down)]),
        "ident": np.eye(P, dtype=f32),
        "consts": consts,
        "iota_t": np.broadcast_to(np.arange(P, dtype=f32), (P, P)),
        "tri": tri,
        "resets": resets,
        "iota_e": np.broadcast_to(iota_e, (P, 2, NE)),
        "rows_to": np.arange(K * N, dtype=f32).reshape(K, R, P).transpose(2, 0, 1),
    }
    arrays = {"in_" + n: np.ascontiguousarray(a) for n, a in arrays.items()}
    nc = bacc.Bacc("TRN2", target_bir_lowering=False, num_devices=1)
    args = [nc.dram_tensor(n, a.shape, mybir.dt.from_np(a.dtype), kind="ExternalInput").ap() for n, a in arrays.items()]
    out = nc.dram_tensor("out", [P, R, D], F32, kind="ExternalOutput").ap()
    build(nc, *args, out)
    got = run_bass_kernel_spmd(nc, [arrays], core_ids=[0]).results[0]["out"]
    return got.reshape(P, B, TB, D).transpose(1, 2, 0, 3).reshape(B, S, D)
```
